# Optimizing a Trainium2 kernel written in Bass

```python
import numpy as np
import jax
import jax.numpy as jnp

def _softmax(x, axis=-1):
    return jax.nn.softmax(x, axis=axis)

def _gelu(x):
    return jax.nn.gelu(x, approximate=True)

def _silu(x):
    return jax.nn.silu(x)

def _sigmoid(x):
    return jax.nn.sigmoid(x)

def _layernorm(x, axis=-1, eps=1e-05):
    m = jnp.mean(x, axis=axis, keepdims=True)
    v = jnp.var(x, axis=axis, keepdims=True)
    return (x - m) / jnp.sqrt(v + eps)

def _scatter_add(tgt, idx, src, axis=0):
    return tgt.at[idx].add(src)

def _segment_sum(src, seg, n):
    return jax.ops.segment_sum(src, seg, n)
kernel_name = 'mk_lm_tower_d1_tok_ids1024_r4_413bc0'

def setup_inputs(seed: int=0):
    np.random.seed(seed)
    _w = jnp.asarray

    def _rec_inputs():
        import jax
        import jax.numpy as jnp
        _rk = jax.random.key(seed)
        x = jax.random.randint(jax.random.fold_in(_rk, 1), (8, 512), 0, 500, jnp.int32)
        return x
    x = _rec_inputs()

    def _L0_tok_setup():
        import jax, jax.numpy as jnp
        import numpy as np
        DIM = 256
        MAX_SEQ_LEN = 500
        KERNEL = 31
        B, N = (32, 500)
        key = jax.random.key(seed)
        k1, k2, k3, k4 = jax.random.split(key, 4)
        x = jax.random.randint(k1, (B, N), 0, MAX_SEQ_LEN)
        embed_table = jax.random.normal(k2, (MAX_SEQ_LEN, DIM), dtype=jnp.float32)
        bound = 1.0 / np.sqrt(KERNEL)
        conv_w = jax.random.uniform(k3, (DIM, 1, KERNEL), minval=-bound, maxval=bound, dtype=jnp.float32)
        conv_b = jax.random.uniform(k4, (DIM,), minval=-bound, maxval=bound, dtype=jnp.float32)
        return {'x': x, 'embed_table': embed_table, 'conv_w': conv_w, 'conv_b': conv_b}
    _L0_tok_all = _L0_tok_setup()
    _L0_tok_in = {k: v for k, v in _L0_tok_all.items() if k in ('embed_table', 'conv_w', 'conv_b')}
    del _L0_tok_all

    def _L0_attn_setup():
        import jax, jax.numpy as jnp
        import numpy as np
        HEADS = 16
        DIM_HEAD = 64
        SCALE = DIM_HEAD ** (-0.5)
        key = jax.random.key(seed)
        k1, k2, k3 = jax.random.split(key, 3)
        B, N, D = (4, 2048, 256)
        inner = HEADS * DIM_HEAD
        x = jax.random.normal(k1, (B, N, D), dtype=jnp.float32)
        w_qkv = jax.random.normal(k2, (D, 3 * inner), dtype=jnp.float32) * D ** (-0.5)
        w_out = jax.random.normal(k3, (inner, D), dtype=jnp.float32) * inner ** (-0.5)
        b_out = jnp.zeros((D,), dtype=jnp.float32)
        return {'x': x, 'w_qkv': w_qkv, 'w_out': w_out, 'b_out': b_out}
    _L0_attn_all = _L0_attn_setup()
    _L0_attn_in = {k: v for k, v in _L0_attn_all.items() if k in ('w_qkv', 'w_out', 'b_out')}
    del _L0_attn_all

    def _L0_ffn_setup():
        import jax, jax.numpy as jnp
        import numpy as np
        N_EMBD = 256
        EXPERT_SIZES = [(4, 256), (4, 512)]
        TOP_K = 2
        B, S = (1, 512)
        WIDTHS = []
        for count, size in EXPERT_SIZES:
            WIDTHS += [size] * count
        OFFSETS = np.concatenate([[0], np.cumsum(WIDTHS)]).astype(np.int64)
        E = len(WIDTHS)
        TOTAL_W = int(OFFSETS[-1])
        MAX_W = max(WIDTHS)

        def _stack_experts(w1, w2):
            W1e, W2e = ([], [])
            for e in range(E):
                off, wd = (int(OFFSETS[e]), WIDTHS[e])
                pad = MAX_W - wd
                W1e.append(jnp.pad(w1[:, off:off + wd], ((0, 0), (0, pad))))
                W2e.append(jnp.pad(w2[off:off + wd, :], ((0, pad), (0, 0))))
            return (jnp.stack(W1e), jnp.stack(W2e))
        key = jax.random.key(seed)
        k1, k2, k3, k4 = jax.random.split(key, 4)
        x = jax.random.normal(k1, (B, S, N_EMBD), jnp.float32)
        router_w = jax.random.normal(k2, (E, N_EMBD), jnp.float32) * 0.02
        w1 = jax.random.truncated_normal(k3, -3.0, 3.0, (N_EMBD, TOTAL_W), jnp.float32) * 0.02
        w2 = jax.random.truncated_normal(k4, -3.0, 3.0, (TOTAL_W, N_EMBD), jnp.float32) * 0.02
        return {'x': x, 'router_w': router_w, 'w1': w1, 'w2': w2}
    _L0_ffn_all = _L0_ffn_setup()
    _L0_ffn_in = {k: v for k, v in _L0_ffn_all.items() if k in ('router_w', 'w1', 'w2')}
    del _L0_ffn_all
    return {'x': x, 'L0_tok_embed_table': _L0_tok_in['embed_table'], 'L0_tok_conv_w': _L0_tok_in['conv_w'], 'L0_tok_conv_b': _L0_tok_in['conv_b'], 'L0_attn_w_qkv': _L0_attn_in['w_qkv'], 'L0_attn_w_out': _L0_attn_in['w_out'], 'L0_attn_b_out': _L0_attn_in['b_out'], 'L0_ffn_router_w': _L0_ffn_in['router_w'], 'L0_ffn_w1': _L0_ffn_in['w1'], 'L0_ffn_w2': _L0_ffn_in['w2']}

def reference(x, L0_tok_embed_table, L0_tok_conv_w, L0_tok_conv_b, L0_attn_w_qkv, L0_attn_w_out, L0_attn_b_out, L0_ffn_router_w, L0_ffn_w1, L0_ffn_w2):
    import jax
    import jax.numpy as jnp

    def _L0_tok_ref(x, embed_table, conv_w, conv_b):
        import jax, jax.numpy as jnp
        import numpy as np
        DIM = 256
        MAX_SEQ_LEN = 500
        KERNEL = 31
        B, N = (32, 500)
        y = embed_table[x]
        y = jnp.transpose(y, (0, 2, 1))
        y = jax.lax.conv_general_dilated(y, conv_w, window_strides=(1,), padding='SAME', dimension_numbers=('NCH', 'OIH', 'NCH'), feature_group_count=DIM)
        y = y + conv_b[None, :, None]
        return jnp.transpose(y, (0, 2, 1))

    def _L0_attn_ref(x, w_qkv, w_out, b_out):
        import jax, jax.numpy as jnp
        import numpy as np
        HEADS = 16
        DIM_HEAD = 64
        SCALE = DIM_HEAD ** (-0.5)
        B, N, D = x.shape
        h, d = (HEADS, DIM_HEAD)
        qkv = x @ w_qkv
        q, k, v = jnp.split(qkv, 3, axis=-1)

        def to_heads(t):
            return t.reshape(B, N, h, d).transpose(0, 2, 1, 3).reshape(B * h, N, d)
        q, k, v = map(to_heads, (q, k, v))
        q = jax.nn.softmax(q * SCALE, axis=-1)
        k = jax.nn.softmax(k, axis=-2)
        context = jnp.einsum('bnd,bne->bde', q, k)
        out = jnp.einsum('bde,bnd->bne', context, v)
        out = out.reshape(B, h, N, d).transpose(0, 2, 1, 3).reshape(B, N, h * d)
        return out @ w_out + b_out

    def _L0_ffn_ref(x, router_w, w1, w2):
        import jax, jax.numpy as jnp
        import numpy as np
        N_EMBD = 256
        EXPERT_SIZES = [(4, 256), (4, 512)]
        TOP_K = 2
        B, S = (1, 512)
        WIDTHS = []
        for count, size in EXPERT_SIZES:
            WIDTHS += [size] * count
        OFFSETS = np.concatenate([[0], np.cumsum(WIDTHS)]).astype(np.int64)
        E = len(WIDTHS)
        TOTAL_W = int(OFFSETS[-1])
        MAX_W = max(WIDTHS)

        def _stack_experts(w1, w2):
            W1e, W2e = ([], [])
            for e in range(E):
                off, wd = (int(OFFSETS[e]), WIDTHS[e])
                pad = MAX_W - wd
                W1e.append(jnp.pad(w1[:, off:off + wd], ((0, 0), (0, pad))))
                W2e.append(jnp.pad(w2[off:off + wd, :], ((0, pad), (0, 0))))
            return (jnp.stack(W1e), jnp.stack(W2e))
        b, s, d = x.shape
        xf = x.reshape(-1, d)
        logits = xf @ router_w.T
        probs = jax.nn.sigmoid(logits.astype(jnp.float32))
        topw, sel = jax.lax.top_k(probs, TOP_K)
        topw = topw / (topw.sum(-1, keepdims=True) + 1e-20)
        topw = topw.astype(x.dtype)
        onehot = sel[:, :, None] == jnp.arange(E)[None, None, :]
        combine = jnp.sum(topw[:, :, None] * onehot, axis=1)
        W1e, W2e = _stack_experts(w1, w2)
        h = jnp.einsum('td,edw->tew', xf, W1e)
        h = jnp.square(jax.nn.relu(h))
        y = jnp.einsum('tew,ewd->ted', h, W2e)
        out = jnp.einsum('ted,te->td', y, combine)
        return out.reshape(b, s, d)
    h = _L0_tok_ref(x, L0_tok_embed_table, L0_tok_conv_w, L0_tok_conv_b)
    h = h + _L0_attn_ref(_layernorm(h, axis=-1), L0_attn_w_qkv, L0_attn_w_out, L0_attn_b_out)
    h = h + _L0_ffn_ref(_layernorm(h, axis=-1), L0_ffn_router_w, L0_ffn_w1, L0_ffn_w2)
    return h

_drawn_inputs = setup_inputs


def setup_inputs(seed=0):
    import zlib

    import numpy as np

    out = dict(_drawn_inputs(seed))
    spreads = {'L0_attn_b_out': (0.0, 0.1)}
    factors = {}
    for name, (base, spread) in spreads.items():
        noise = np.random.default_rng([zlib.crc32(name.encode()), seed]).standard_normal(out[name].shape)
        drawn = base * np.exp(spread * noise) if base else spread * noise
        out[name] = jnp.asarray(drawn.astype(out[name].dtype))
    for name, factor in factors.items():
        out[name] = (out[name] * factor).astype(out[name].dtype)
    return out
```

```python
from contextlib import ExitStack

import concourse.bass as bass
from concourse import mybir

F32 = mybir.dt.float32
F32R = mybir.dt.float32r
BF16 = mybir.dt.bfloat16
I32 = mybir.dt.int32
U32 = mybir.dt.uint32
ALU = mybir.AluOpType
ACT = mybir.ActivationFunctionType
AX = mybir.AxisListType.X

P = 128
BATCHES, SEQ, DIM = 8, 512, 256
TOKENS = BATCHES * SEQ
TAPS = 31
PAD = TAPS // 2
HEADS, DH = 16, 64
INNER = HEADS * DH
SCALE = DH ** -0.5
EPS = 1e-5

BLK = 32
CG = P // BLK
NBLK = SEQ // BLK
GROUPS = DIM // CG
SETS = GROUPS // 4
WIN = 2 * BLK
WPAD = 96

KC = DIM // P
TT = SEQ // P
PAIRS = INNER // P

EXPERTS = 8
NARROW_W, MAXW = 256, 512
WIDTHS = [NARROW_W] * 4 + [MAXW] * 4
NARROW = sum(w == NARROW_W for w in WIDTHS)
FC = MAXW // P
TOPK = 2
QROWS = TOKENS + P
FILLER_ROW = EXPERTS * QROWS
ROW = DIM + 2
TILES = 72
AHEAD = 2
TABLE = TILES + AHEAD
SLOTS = 8
TOTAL_W = sum(WIDTHS)


class Batch:

    def __init__(self, n, par, half):
        self.n, self.par, self.half = n, par, half

    def nth(self, per, k):
        return self.n * per + k

    def is_first(self, count):
        return isinstance(self.n, int) and self.n < count


def wait_apart(engine, sem, value, passed):
    engine.wait_ge(sem, value)
    engine.sem_inc(passed, 1)


def unless_none(fn):
    def part(b, *args):
        if b is not None:
            fn(b, *args)
    return part


def on_all(vector):
    return vector.partition_broadcast(P)


def tower(nc, x, table, conv_w, conv_b, w_qkv, w_out, b_out, router_w, w1, w2, out):
    top = ExitStack()
    with top:
        bank = [top.enter_context(nc.psum_tensor(f"bank{i}", [P, 512], F32)) for i in range(8)]

        def sem(name):
            return top.enter_context(nc.semaphore(name))

        def sbuf(stack, name, shape, dt=F32):
            return stack.enter_context(nc.sbuf_tensor(name, shape, dt))

        taps_d = nc.dram_tensor("taps_d", [DIM, WPAD], F32).ap()
        h_d = nc.dram_tensor("h_d", [TOKENS, DIM], F32).ap()
        queue_d = nc.dram_tensor("queue_d", [FILLER_ROW + P, ROW], F32).ap()

        ident = sbuf(top, "ident", [P, P])
        base = sbuf(top, "base", [P, EXPERTS])
        base0 = sbuf(top, "base0", [P, EXPERTS])

        with ExitStack() as attn_ctx:
            wqk_hi = sbuf(attn_ctx, "wqk_hi", [P, KC, 2 * INNER], F32R)
            wqk_lo = sbuf(attn_ctx, "wqk_lo", [P, KC, 2 * INNER], F32R)
            wv_t = sbuf(attn_ctx, "wv_t", [P, PAIRS, DIM])
            wo = sbuf(attn_ctx, "wo", [P, PAIRS, DIM])
            bo_all = sbuf(attn_ctx, "bo_all", [P, DIM])
            with ExitStack() as conv_ctx:
                convolve(nc, conv_ctx, sem, bank, ident, x, table, conv_w, conv_b, w_qkv, w_out, b_out,
                         taps_d, h_d, wqk_hi, wqk_lo, wv_t, wo, bo_all)
            with ExitStack() as ctx:
                attend(nc, ctx, sem, bank, ident, base, base0, router_w, h_d, queue_d, out,
                       wqk_hi, wqk_lo, wv_t, wo, bo_all)
        with ExitStack() as ctx:
            experts(nc, ctx, sem, bank, ident, base, base0, w1, w2, queue_d, out)


def convolve(nc, ctx, sem, bank, ident, x, table, conv_w, conv_b, w_qkv, w_out, b_out,
             taps_d, h_d, wqk_hi, wqk_lo, wv_t, wo, bo_all):
    def sbuf(name, shape, dt=F32):
        return ctx.enter_context(nc.sbuf_tensor(name, shape, dt))

    ids = sbuf("ids", [P, BLK], I32)
    rows = sbuf("rows", [P, BLK, DIM])
    turned = sbuf("turned", [P, 4, 4, NBLK + 1, BATCHES])
    taps = sbuf("taps", [P, KC, TAPS])
    padded = sbuf("padded", [P, KC, WPAD])
    windows = sbuf("windows", [P, GROUPS, WIN])
    banded = sbuf("banded", [P, 2, 16, WIN, CG])
    same_ch = sbuf("same_ch", [P, CG])
    head_rows = sbuf("head_rows", [P, 1])
    tail_rows = sbuf("tail_rows", [P, 1])
    cb_all = sbuf("cb_all", [P, DIM])
    h = sbuf("h", [P, BLK, DIM])
    wqk = sbuf("wqk", [P, KC, 2 * INNER])
    wv = sbuf("wv", [P, KC, INNER])

    ids_in, taps_in, bias_in, wqk_in, wv_in, wo_in = (sem(n) for n in (
        "ids_in", "taps_in", "bias_in", "wqk_in", "wv_in", "wo_in"))
    taps_out, windows_sp, windows_act, gathered = (sem(n) for n in (
        "taps_out", "windows_sp", "windows_act", "gathered"))
    padded_zero, padded_ready, ident_zero, ident_ready, masks_ready = (sem(n) for n in (
        "padded_zero", "padded_ready", "ident_zero", "ident_ready", "masks_ready"))
    rows_turned, turned_ready, banded_ready, conv_done, conv_added = (sem(n) for n in (
        "rows_turned", "turned_ready", "banded_ready", "conv_done", "conv_added"))
    h_stored = sem("h_stored")
    wqk_hi_ready, wqk_lo_ready, wv_turned, wv_copied = (sem(n) for n in (
        "wqk_hi_ready", "wqk_lo_ready", "wv_turned", "wv_copied"))

    taps_v = taps_d.rearrange("(c g) j -> c g j", c=CG)
    h_v = h_d.rearrange("(b s o) c -> s b (o c)", b=BATCHES, o=BLK)

    def load_window(eng, i, done):
        return eng.dma_start(windows[CG * i:CG * i + CG, :, :],
                             taps_v[:, :, 31 - i:31 - i + WIN]).then_inc(done, 16)

    with nc.Block() as block:
        @block.sync
        def _(sp):
            sp.dma_start(ids[:], x).then_inc(ids_in, 16)
            sp.dma_start(taps[:], conv_w.rearrange("(p a) o k -> p a (o k)", a=KC)).then_inc(taps_in, 16)
            sp.wait_ge(padded_ready, 1)
            sp.dma_start(taps_d.rearrange("(p a) j -> p a j", a=KC), padded[:]).then_inc(taps_out, 16)
            sp.wait_ge(taps_out, 16)
            for i in range(0, BLK, 2):
                load_window(sp, i, windows_sp)
            sp.dma_start(cb_all[:], on_all(conv_b)).then_inc(bias_in, 16)
            sp.dma_start(wqk[:], w_qkv.rearrange("(k p) n -> p k n", p=P)[:, :, 0:2 * INNER]).then_inc(wqk_in, 16)
            sp.dma_start(wv[:], w_qkv.rearrange("(k p) n -> p k n", p=P)[:, :, 2 * INNER:3 * INNER]
                         ).then_inc(wv_in, 16)
            sp.dma_start(wo[:], w_out.rearrange("(a p) n -> p a n", p=P)).then_inc(wo_in, 16)
            sp.dma_start(bo_all[:], on_all(b_out)).then_inc(wo_in, 16)
            sp.wait_ge(conv_added, SETS)
            for n in range(4):
                sp.dma_start(h_v[4 * n:4 * n + 4], h[32 * n:32 * n + 32].rearrange("p o c -> p (o c)")
                             ).then_inc(h_stored, 16)
            sp.wait_ge(h_stored, 64)
            sp.wait_ge(wo_in, 32)

        @block.gpsimd
        def _(pool):
            nc.gpsimd.memset(ident[:], 0.0).then_inc(ident_zero, 1)
            pool.wait_ge(ident_zero, 1)
            nc.gpsimd.affine_select(out=ident[:], in_=ident[:], compare_op=ALU.not_equal, fill=1.0, base=0,
                                    pattern=[[-1, P]], channel_multiplier=1).then_inc(ident_ready, 1)
            pool.wait_ge(ids_in, 16)
            for i in range(BLK):
                pool.indirect_dma_start(out=rows[:, i, :], out_offset=None, in_=table,
                                        in_offset=bass.IndirectOffsetOnAxis(ap=ids[:, i:i + 1].bitcast(U32), axis=0)
                                        ).then_inc(gathered, 16)
            for k in range(KC):
                pool.wait_ge(wqk_hi_ready, k + 1)
                nc.gpsimd.tensor_tensor(wqk_lo[:, k], wqk[:, k], wqk_hi[:, k].bitcast(F32), ALU.subtract
                                        ).then_inc(wqk_lo_ready, 1)

        @block.scalar
        def _(act):
            act.wait_ge(taps_out, 16)
            for i in range(1, BLK, 2):
                load_window(act, i, windows_act)

            def make_banded(q):
                if q >= 2:
                    act.wait_ge(conv_done, 4 * (q - 1))
                for c in range(CG):
                    last = nc.scalar.activation(banded[:, q % 2, :, :, c], windows[:, 16 * q:16 * q + 16, :],
                                                ACT.Copy, scale=same_ch[:, c:c + 1])
                last.then_inc(banded_ready, 1)

            act.wait_ge(windows_sp, 16 * (BLK // 2))
            act.wait_ge(windows_act, 16 * (BLK // 2))
            act.wait_ge(masks_ready, 3)
            make_banded(0)
            make_banded(1)
            act.wait_ge(wqk_in, 16)
            for k in range(KC):
                nc.scalar.activation(wqk_hi[:, k], wqk[:, k], ACT.Copy).then_inc(wqk_hi_ready, 1)
            make_banded(2)
            make_banded(3)

        @block.vector
        def _(dve):
            nc.vector.memset(padded[:], 0.0).then_inc(padded_zero, 1)
            dve.wait_ge(padded_zero, 1)
            dve.wait_ge(taps_in, 16)
            nc.vector.tensor_copy(padded[:, :, 33:33 + TAPS], taps[:, :, ::-1]).then_inc(padded_ready, 1)
            dve.wait_ge(ident_ready, 1)
            nc.vector.tensor_reduce(same_ch[:], ident[:].rearrange("p (i c) -> p c i", c=CG), AX, ALU.add
                                    ).then_inc(masks_ready, 1)
            nc.vector.tensor_reduce(tail_rows[:], ident[:, 0:CG * PAD], AX, ALU.add).then_inc(masks_ready, 1)
            nc.vector.tensor_reduce(head_rows[:], ident[:, CG * PAD:P], AX, ALU.add).then_inc(masks_ready, 1)
            dve.wait_ge(masks_ready, 3)

            def take_turned(s):
                dve.wait_ge(rows_turned, s + 1)
                src = bank[s % 4][:].rearrange("p (g s b) -> p g s b", g=4, s=NBLK)
                dst = turned[:, s % 4]
                nc.vector.tensor_copy(dst[:, :, 1:NBLK], src[:, :, 1:NBLK])
                nc.vector.tensor_scalar(dst[:, :, 0], src[:, :, 0], head_rows[:, 0:1], None, ALU.mult)
                nc.vector.tensor_scalar(dst[:, :, NBLK], src[:, :, 0], tail_rows[:, 0:1], None, ALU.mult
                                        ).then_inc(turned_ready, 1)

            def add_bias(s):
                dve.wait_ge(conv_done, s + 1)
                if s == 0:
                    dve.wait_ge(bias_in, 16)
                src = bank[4 + s % 4][:].rearrange("p (g o c) -> p g o c", g=4, c=CG)
                dst = h[:].rearrange("p o (c g) -> p g o c", c=CG)[:, 4 * s:4 * s + 4]
                bias = cb_all[:].rearrange("p (c g) -> p g c", c=CG)[:, 4 * s:4 * s + 4].unsqueeze(2
                    ).to_broadcast([P, 4, BLK, CG])
                nc.vector.tensor_tensor(dst, src, bias, ALU.add).then_inc(conv_added, 1)

            take_turned(0)
            take_turned(1)
            for s in range(SETS):
                if s + 2 < SETS:
                    take_turned(s + 2)
                add_bias(s)
            for n in range(4):
                dve.wait_ge(wv_turned, n + 1)
                nc.vector.tensor_copy(wv_t[:, 2 * n:2 * n + 2, :],
                                      bank[n][:].rearrange("p (a k) -> p a k", a=2)).then_inc(wv_copied, 1)

        @block.tensor
        def _(pe):
            def turn(s):
                if s >= 4:
                    pe.wait_ge(turned_ready, s - 3)
                for g in range(4):
                    last = nc.tensor.transpose(bank[s % 4][:, P * g:P * g + P],
                                               rows[:].rearrange("p i (c g) -> p g (i c)", c=CG)[:, 4 * s + g],
                                               ident[:])
                last.then_inc(rows_turned, 1)

            def conv(s):
                pe.wait_ge(turned_ready, s + 1)
                pe.wait_ge(banded_ready, s // 4 + 1)
                if s >= 4:
                    pe.wait_ge(conv_added, s - 3)
                for g in range(4):
                    o = bank[4 + s % 4][:, P * g:P * g + P]
                    cols = turned[:, s % 4, g].rearrange("p s b -> p (s b)")
                    m = banded[:, (s // 4) % 2, 4 * (s % 4) + g]
                    nc.tensor.matmul(o, cols[:, 0:P], m[:, BLK:WIN], start=True, stop=False)
                    last = nc.tensor.matmul(o, cols[:, BATCHES:BATCHES + P], m[:, 0:BLK],
                                            start=False, stop=True)
                last.then_inc(conv_done, 1)

            pe.wait_ge(ident_ready, 1)
            pe.wait_ge(gathered, 16 * BLK)
            turn(0)
            turn(1)
            for s in range(SETS):
                if s + 2 < SETS:
                    turn(s + 2)
                conv(s)
            pe.wait_ge(wv_in, 16)
            pe.wait_ge(turned_ready, SETS)
            for n in range(4):
                for a in range(2):
                    for k in range(KC):
                        last = nc.tensor.transpose(bank[n][:, 256 * a + P * k:256 * a + P * k + P],
                                                   wv[:, k, P * (2 * n + a):P * (2 * n + a) + P], ident[:])
                last.then_inc(wv_turned, 1)


def attend(nc, ctx, sem, bank, ident, base, base0, router_w, h_d, queue_d, out,
           wqk_hi, wqk_lo, wv_t, wo, bo_all):
    def sbuf(name, shape, dt=F32):
        return ctx.enter_context(nc.sbuf_tensor(name, shape, dt))

    h_in = sbuf("h_in", [P, 2, TT, DIM])
    res = sbuf("res", [P, 2, TT, DIM])
    xn = sbuf("xn", [P, TT, DIM])
    xt_hi = sbuf("xt_hi", [P, 2, KC, SEQ], F32R)
    xt_lo = sbuf("xt_lo", [P, 2, KC, SEQ], F32R)
    q = sbuf("q", [P, 2, TT, INNER])
    q_max = sbuf("q_max", [P, 2, 8])
    q_sum = sbuf("q_sum", [P, 2, 8])
    q_inv = sbuf("q_inv", [P, 2, 2 * TT, 8])
    k_negmax = sbuf("k_negmax", [P, PAIRS])
    k_exps = sbuf("k_exps", [P, 2, SEQ])
    k_sum = sbuf("k_sum", [P, 2, PAIRS])
    k_inv = sbuf("k_inv", [P, PAIRS])
    k = sbuf("k", [P, TT, INNER])
    context = sbuf("context", [P, PAIRS, P])
    g = sbuf("g", [P, PAIRS, DIM])
    m_hi = sbuf("m_hi", [P, KC, DIM], F32R)
    m_lo = sbuf("m_lo", [P, KC, DIM], F32R)
    stats = sbuf("stats", [P, TT, 6])
    mean_var = sbuf("mean_var", [P, TT, 2])
    var_eps = sbuf("var_eps", [P, TT])
    rstd = sbuf("rstd", [P, TT])
    minus_half = sbuf("minus_half", [P, TT])
    stats2 = sbuf("stats2", [P, TT, 6])
    mean_var2 = sbuf("mean_var2", [P, TT, 2])
    var_eps2 = sbuf("var_eps2", [P, TT])
    rstd2 = sbuf("rstd2", [P, TT])
    x2_t = sbuf("x2_t", [P, KC, SEQ])
    row = sbuf("row", [P, TT, TOPK, ROW])
    rw = sbuf("rw", [EXPERTS, DIM])
    rw_t = sbuf("rw_t", [P, KC, EXPERTS])
    prob = sbuf("prob", [P, TT, EXPERTS])
    best = sbuf("best", [P, TT, 8])
    best_at = sbuf("best_at", [P, TT, 8], U32)
    best_atf = sbuf("best_atf", [P, TOPK, TT])
    top_sum = sbuf("top_sum", [P, TT])
    which = sbuf("which", [P, TOPK * TT, EXPERTS])
    counted = sbuf("counted", [P, TT * EXPERTS], BF16)
    place = sbuf("place", [P, TT, EXPERTS])
    placed = sbuf("placed", [P, TOPK * TT, EXPERTS])
    slotf = sbuf("slotf", [P, TOPK * TT])
    slot = sbuf("slot", [P, TOPK * TT], U32)
    before = sbuf("before", [P, P], BF16)
    every = sbuf("every", [P, P], BF16)
    expert_no = sbuf("expert_no", [P, EXPERTS])
    token_no = sbuf("token_no", [P, TT])

    loaded = [sem(f"loaded{i}") for i in range(2)]
    stored = [sem(f"stored{i}") for i in range(2)]
    consts_pool, rw_in, rw_turned, rw_copied = (
        sem(n) for n in ("consts_pool", "rw_in", "rw_turned", "rw_copied"))
    ln_chain, stats_ready, var_ready, rstd_ready, xn_ready = (
        sem(n) for n in ("ln_chain", "stats_ready", "var_ready", "rstd_ready", "xn_ready"))
    res_ready, qk_psum, xt_hi_ready, xt_lo_ready, q_chain = (
        sem(n) for n in ("res_ready", "qk_psum", "xt_hi_ready", "xt_lo_ready", "q_chain"))
    q_shifted, q_exp_ready, q_inv_ready, q_ready, k_max_ready = (
        sem(n) for n in ("q_shifted", "q_exp_ready", "q_inv_ready", "q_ready", "k_max_ready"))
    k_exp_ready, k_psum, k_ready, tail_chain, tail_psum = (
        sem(n) for n in ("k_exp_ready", "k_psum", "k_ready", "tail_chain", "tail_psum"))
    ctx_ready, g_ready, m_hi_ready, m_lo_ready, res_added = (
        sem(n) for n in ("ctx_ready", "g_ready", "m_hi_ready", "m_lo_ready", "res_added"))
    stats2_ready, var2_ready, rstd2_ready, row_ready, x2t_ready = (
        sem(n) for n in ("stats2_ready", "var2_ready", "rstd2_ready", "row_ready", "x2t_ready"))
    prob_exp_ready, counted_ready, rank_psum, slots_ready, queued = (
        sem(n) for n in ("prob_exp_ready", "counted_ready", "rank_psum", "slots_ready", "queued"))
    dve_passed, pool_passed = (
        sem(n) for n in ("dve_passed", "pool_passed"))

    QK_USES, Q_UNITS, TAIL_USES = 2 + 2 * TT + PAIRS, 2 * TT, 12
    LN_LINKS, Q_LINKS, BEST_LINKS, TAIL_LINKS = 1, 2 * Q_UNITS, 8, 17

    def qk_bank(use):
        return bank[use % 3]

    def k_bank(c):
        return bank[3 + c % 2]

    def tail_bank(use):
        return bank[5 + use % 3]

    def steps(engine, step):
        b = [Batch(n, n % 2, n // 2) for n in range(BATCHES)]
        step(None, None, b[0], None)
        step(b[0], None, b[1], None)
        step(b[1], b[0], b[2], None)
        with engine.Fori(1, BATCHES // 2) as i:
            even, odd = Batch(i * 2, 0, i), Batch(i * 2 + 1, 1, i)
            step(even, Batch(i * 2 - 1, 1, i - 1), odd, Batch(i * 2 - 2, 0, i - 1))
            step(odd, even, Batch(i * 2 + 2, 0, i + 1), Batch(i * 2 - 1, 1, i - 1))
        step(None, b[BATCHES - 1], None, b[BATCHES - 2])
        step(None, None, None, b[BATCHES - 1])

    with nc.Block() as block:
        @block.sync
        def _(sp):
            sp.dma_start(rw[:], router_w).then_inc(rw_in, 16)

            @unless_none
            def load(b):
                if not (b.is_first(2)):
                    sp.wait_ge(xn_ready, b.nth(1, -1))
                    sp.wait_ge(res_ready, b.nth(1, -1))
                first = b.n * SEQ if isinstance(b.n, int) else (b.n % BATCHES) * SEQ
                sp.dma_start(h_in[:, b.par], h_d[bass.ds(first, SEQ), :].rearrange("(t p) c -> p t c", p=P)
                             ).then_inc(loaded[b.par], 16)

            @unless_none
            def store(b):
                sp.wait_ge(res_added, b.nth(2, 2))
                sp.dma_start(out[bass.ds(b.n * SEQ, SEQ), :].rearrange("(t p) c -> p t c", p=P), res[:, b.par]
                             ).then_inc(stored[b.par], 16)

            def step(b, prev, nxt, old):
                load(nxt)
                store(prev)

            steps(sp, step)
            for s in stored:
                sp.wait_ge(s, 16 * BATCHES // 2)

        @block.gpsimd
        def _(pool):
            nc.gpsimd.memset(minus_half[:], -0.5).then_inc(consts_pool, 1)
            nc.gpsimd.memset(before[:], 1.0).then_inc(consts_pool, 1)
            nc.gpsimd.memset(every[:], 1.0).then_inc(consts_pool, 1)
            nc.gpsimd.memset(context[:], 0.0).then_inc(consts_pool, 1)
            nc.gpsimd.iota(expert_no[:], [[1, EXPERTS]], base=0, channel_multiplier=0,
                           allow_small_or_imprecise_dtypes=True).then_inc(consts_pool, 1)
            nc.gpsimd.iota(base0[:], [[QROWS, EXPERTS]], base=0, channel_multiplier=0,
                           allow_small_or_imprecise_dtypes=True).then_inc(consts_pool, 1)
            nc.gpsimd.iota(base[:], [[QROWS, EXPERTS]], base=0, channel_multiplier=0,
                           allow_small_or_imprecise_dtypes=True).then_inc(consts_pool, 1)
            nc.gpsimd.iota(token_no[:], [[P, TT]], base=0, channel_multiplier=1,
                           allow_small_or_imprecise_dtypes=True).then_inc(consts_pool, 1)
            pool.wait_ge(consts_pool, 8)
            nc.gpsimd.affine_select(out=before[:], in_=before[:], compare_op=ALU.is_gt, fill=0.0, base=0,
                                    pattern=[[1, P]], channel_multiplier=-1).then_inc(consts_pool, 1)

            @unless_none
            def residual(b):
                pool.wait_ge(loaded[b.par], (b.half + 1) * 16)
                if not (b.is_first(2)):
                    pool.wait_ge(stored[b.par], b.half * 16)
                    pool.wait_ge(row_ready, b.nth(1, -1))
                nc.gpsimd.tensor_tensor(res[:, b.par], h_in[:, b.par],
                                        bo_all[:].unsqueeze(1).to_broadcast([P, TT, DIM]), ALU.add
                                        ).then_inc(res_ready, 1)

            def root(b, mv, ve, r, ready, mid, done):
                wait_apart(pool, ready, b.nth(1, 1), pool_passed)
                nc.gpsimd.tensor_scalar(ve[:], mv[:, :, 1], EPS, None, ALU.add).then_inc(mid, 1)
                pool.wait_ge(mid, b.nth(1, 1))
                nc.gpsimd.tensor_tensor(r[:], ve[:], minus_half[:], ALU.pow).then_inc(done, 1)

            @unless_none
            def root1(b):
                root(b, mean_var, var_eps, rstd, stats_ready, var_ready, rstd_ready)

            @unless_none
            def root2(b):
                root(b, mean_var2, var_eps2, rstd2, stats2_ready, var2_ready, rstd2_ready)

            @unless_none
            def q_norm(b, u):
                pool.wait_ge(q_inv_ready, b.nth(Q_UNITS, u + 1))
                v = q[:, b.par, u // 2, 512 * (u % 2):512 * (u % 2) + 512].rearrange("p (h d) -> p h d", d=DH)
                nc.gpsimd.tensor_tensor(v, v, q_inv[:, b.par, u].unsqueeze(2).to_broadcast([P, 8, DH]), ALU.mult
                                        ).then_inc(q_ready, 1)

            @unless_none
            def enqueue(b):
                wait_apart(pool, slots_ready, b.nth(1, 1), pool_passed)
                for c in range(TOPK):
                    for t in range(TT):
                        pool.indirect_dma_start(
                            out=queue_d, in_=row[:, t, c, :], in_offset=None,
                            out_offset=bass.IndirectOffsetOnAxis(ap=slot[:, TT * c + t:TT * c + t + 1], axis=0)
                        ).then_inc(queued, 16)

            def step(b, prev, nxt, old):
                enqueue(old)
                q_norm(b, 0)
                q_norm(b, 1)
                q_norm(b, 2)
                q_norm(b, 3)
                q_norm(b, 4)
                q_norm(b, 5)
                q_norm(b, 6)
                q_norm(b, 7)
                root1(nxt)
                root2(prev)
                residual(nxt)

            steps(pool, step)
            pool.wait_ge(queued, 16 * TOPK * TT * BATCHES)

        @block.scalar
        def _(act):
            def copy(dst, src, waits, done):
                for s, v in waits:
                    act.wait_ge(s, v)
                nc.scalar.activation(dst, src, ACT.Copy).then_inc(done, 1)

            @unless_none
            def xt_high(b, kk):
                copy(xt_hi[:, b.par, kk], qk_bank(kk)[:], [(qk_psum, b.nth(QK_USES, kk + 1))], xt_hi_ready)

            @unless_none
            def q_exps(b, u):
                act.wait_ge(q_shifted, b.nth(Q_UNITS, u + 1))
                v = q[:, b.par, u // 2, 512 * (u % 2):512 * (u % 2) + 512]
                nc.scalar.activation(v, v, ACT.Exp, scale=SCALE).then_inc(q_exp_ready, 1)

            @unless_none
            def k_exp(b, c):
                act.wait_ge(k_max_ready, b.nth(PAIRS, c + 1))
                if c >= 2 or not (b.is_first(1)):
                    act.wait_ge(k_psum, b.nth(PAIRS, c - 1))
                nc.scalar.activation(k_exps[:, c % 2], qk_bank(10 + c)[:], ACT.Exp, bias=k_negmax[:, c:c + 1],
                                     accum_out=k_sum[:, b.par, c:c + 1]).then_inc(k_exp_ready, 1)

            @unless_none
            def k_take(b, c):
                copy(k[:, :, P * c:P * c + P], k_bank(c)[:].rearrange("p (t e) -> p t e", t=TT),
                     [(k_psum, b.nth(PAIRS, c + 1))], k_ready)

            @unless_none
            def g_take(b, n):
                copy(g[:, 2 * n:2 * n + 2], tail_bank(2 + n)[:].rearrange("p (a n) -> p a n", a=2),
                     [(tail_psum, b.nth(TAIL_USES, 3 + n))], g_ready)

            @unless_none
            def m_high(b):
                copy(m_hi[:], tail_bank(6)[:].rearrange("p (a n) -> p a n", a=2),
                     [(tail_psum, b.nth(TAIL_USES, 7))], m_hi_ready)

            @unless_none
            def x2_take(b, kk):
                copy(x2_t[:, kk], tail_bank(9 + kk)[:], [(tail_psum, b.nth(TAIL_USES, 10 + kk))], x2t_ready)

            @unless_none
            def prob_exp(b):
                act.wait_ge(tail_psum, b.nth(TAIL_USES, 12))
                nc.scalar.activation(prob[:].rearrange("p t e -> p (t e)"), tail_bank(11)[:, 0:TT * EXPERTS],
                                     ACT.Exp, scale=-1.0).then_inc(prob_exp_ready, 1)

            def step(b, prev, nxt, old):
                q_exps(b, 0)
                q_exps(b, 1)
                q_exps(b, 2)
                q_exps(b, 3)
                g_take(prev, 0)
                q_exps(b, 4)
                g_take(prev, 1)
                q_exps(b, 5)
                g_take(prev, 2)
                q_exps(b, 6)
                g_take(prev, 3)
                q_exps(b, 7)
                k_exp(b, 0)
                m_high(prev)
                k_exp(b, 1)
                k_take(b, 0)
                k_exp(b, 2)
                k_exp(b, 3)
                k_take(b, 1)
                k_exp(b, 4)
                k_take(b, 2)
                k_exp(b, 5)
                k_take(b, 3)
                x2_take(prev, 0)
                x2_take(prev, 1)
                k_exp(b, 6)
                k_take(b, 4)
                k_exp(b, 7)
                k_take(b, 5)
                xt_high(nxt, 0)
                xt_high(nxt, 1)
                prob_exp(prev)
                k_take(b, 6)
                k_take(b, 7)

            steps(act, step)

        @block.vector
        def _(dve):
            dve.wait_ge(rw_turned, 1)
            nc.vector.tensor_copy(rw_t[:], bank[0][:, 0:KC * EXPERTS].rearrange("p (k e) -> p k e", k=KC)
                                  ).then_inc(rw_copied, 1)
            dve.wait_ge(consts_pool, 9)

            def link(ins, chain, b, per, n, apart=False):
                ins.then_inc(chain, 1)
                if apart:
                    wait_apart(dve, chain, b.nth(per, n), dve_passed)
                else:
                    dve.wait_ge(chain, b.nth(per, n))

            @unless_none
            def ln_stats(b):
                dve.wait_ge(loaded[b.par], (b.half + 1) * 16)
                for t in range(TT):
                    last = nc.vector.bn_stats(stats[:, t], h_in[:, b.par, t])
                link(last, ln_chain, b, LN_LINKS, 1, apart=True)
                for t in range(TT):
                    last = nc.vector.bn_aggr(mean_var[:, t], stats[:, t])
                last.then_inc(stats_ready, 1)

            @unless_none
            def ln_apply(b):
                dve.wait_ge(rstd_ready, b.nth(1, 1))
                if not (b.is_first(1)):
                    dve.wait_ge(qk_psum, b.nth(QK_USES, 2 - QK_USES))
                for t in range(TT):
                    last = nc.vector.tensor_scalar(xn[:, t], h_in[:, b.par, t], mean_var[:, t, 0:1], rstd[:, t:t + 1],
                                                   ALU.subtract, ALU.mult)
                last.then_inc(xn_ready, 1)

            @unless_none
            def xt_low(b, kk):
                dve.wait_ge(xt_hi_ready, b.nth(KC, kk + 1))
                nc.vector.tensor_tensor(xt_lo[:, b.par, kk], qk_bank(kk)[:], xt_hi[:, b.par, kk].bitcast(F32),
                                        ALU.subtract).then_inc(xt_lo_ready, 1)

            @unless_none
            def q_shift(b, u):
                dve.wait_ge(qk_psum, b.nth(QK_USES, u + 3))
                src = qk_bank(2 + u)[:].rearrange("p (h d) -> p h d", d=DH)
                link(nc.vector.tensor_reduce(q_max[:, u % 2], src, AX, ALU.max), q_chain, b, Q_LINKS, 2 * u + 1 - (u > 0))
                v = q[:, b.par, u // 2, 512 * (u % 2):512 * (u % 2) + 512].rearrange("p (h d) -> p h d", d=DH)
                nc.vector.tensor_tensor(v, src, q_max[:, u % 2].unsqueeze(2).to_broadcast([P, 8, DH]), ALU.subtract
                                        ).then_inc(q_shifted, 1)

            @unless_none
            def q_total(b, u):
                dve.wait_ge(q_exp_ready, b.nth(Q_UNITS, u + 1))
                v = q[:, b.par, u // 2, 512 * (u % 2):512 * (u % 2) + 512].rearrange("p (h d) -> p h d", d=DH)
                link(nc.vector.tensor_reduce(q_sum[:, u % 2], v, AX, ALU.add), q_chain, b, Q_LINKS,
                     min(2 * u + 3, Q_LINKS))
                nc.vector.reciprocal(q_inv[:, b.par, u], q_sum[:, u % 2]).then_inc(q_inv_ready, 1)

            @unless_none
            def k_max(b, c):
                dve.wait_ge(qk_psum, b.nth(QK_USES, 11 + c))
                if not (b.is_first(1)):
                    dve.wait_ge(k_exp_ready, b.nth(PAIRS, c + 1 - PAIRS))
                nc.vector.tensor_reduce(k_negmax[:, c:c + 1], qk_bank(10 + c)[:], AX, ALU.max, negate=True
                                        ).then_inc(k_max_ready, 1)

            @unless_none
            def context_take(b, n):
                if n == 0:
                    dve.wait_ge(k_exp_ready, b.nth(PAIRS, PAIRS))
                    link(nc.vector.reciprocal(k_inv[:], k_sum[:, b.par]), tail_chain, b, TAIL_LINKS, 1)
                dve.wait_ge(tail_psum, b.nth(TAIL_USES, n + 1))
                for half in range(2):
                    r = slice(DH * half, DH * half + DH)
                    src = tail_bank(n)[r, :].rearrange("p (a d) -> p a d", a=4)[:, :, r]
                    last = nc.vector.tensor_tensor(context[r, 4 * n:4 * n + 4, r], src,
                                                   k_inv[r, 4 * n:4 * n + 4].unsqueeze(2).to_broadcast([DH, 4, DH]),
                                                   ALU.mult)
                last.then_inc(ctx_ready, 1)

            @unless_none
            def m_low(b):
                dve.wait_ge(m_hi_ready, b.nth(1, 1))
                nc.vector.tensor_tensor(m_lo[:], tail_bank(6)[:].rearrange("p (a n) -> p a n", a=2),
                                        m_hi[:].bitcast(F32), ALU.subtract).then_inc(m_lo_ready, 1)

            @unless_none
            def add_attention(b):
                dve.wait_ge(res_ready, b.nth(1, 1))
                for n in range(2):
                    dve.wait_ge(tail_psum, b.nth(TAIL_USES, 8 + n))
                    r = res[:, b.par, 2 * n:2 * n + 2]
                    nc.vector.tensor_tensor(r, tail_bank(7 + n)[:].rearrange("p (t c) -> p t c", t=2), r, ALU.add
                                            ).then_inc(res_added, 1)

            @unless_none
            def ln2_stats(b):
                dve.wait_ge(res_added, b.nth(2, 2))
                for t in range(TT):
                    last = nc.vector.bn_stats(stats2[:, t], res[:, b.par, t])
                link(last, tail_chain, b, TAIL_LINKS, 2, apart=True)
                for t in range(TT):
                    last = nc.vector.bn_aggr(mean_var2[:, t], stats2[:, t])
                last.then_inc(stats2_ready, 1)

            @unless_none
            def ln2_apply(b):
                dve.wait_ge(rstd2_ready, b.nth(1, 1))
                if not (b.is_first(1)):
                    dve.wait_ge(queued, b.nth(16 * TOPK * TT, 0))
                for t in range(TT):
                    last = nc.vector.tensor_scalar(row[:, t, :, 0:DIM],
                                                   res[:, b.par, t].unsqueeze(1).to_broadcast([P, TOPK, DIM]),
                                                   mean_var2[:, t, 0:1], rstd2[:, t:t + 1], ALU.subtract, ALU.mult)
                last.then_inc(row_ready, 1)

            @unless_none
            def route_best(b):
                n = [2]

                def then(ins, apart=False):
                    n[0] += 1
                    link(ins, tail_chain, b, TAIL_LINKS, n[0], apart)

                dve.wait_ge(prob_exp_ready, b.nth(1, 1))
                then(nc.vector.tensor_scalar(prob[:], prob[:], 1.0, None, ALU.add))
                then(nc.vector.reciprocal(prob[:], prob[:]), apart=True)
                for t in range(TT):
                    last = nc.vector.max(best[:, t], prob[:, t])
                then(last, apart=True)
                for t in range(TT):
                    last = nc.vector.max_index(best_at[:, t], best[:, t], prob[:, t])
                then(last)
                then(nc.vector.tensor_copy(best_atf[:], best_at[:, :, 0:TOPK].rearrange("p t c -> p c t")))
                then(nc.vector.tensor_tensor(which[:], expert_no[:].unsqueeze(1).to_broadcast([P, TOPK * TT, EXPERTS]),
                                             best_atf[:].rearrange("p c t -> p (c t)").unsqueeze(2).to_broadcast(
                                                 [P, TOPK * TT, EXPERTS]), ALU.is_equal))
                nc.vector.tensor_tensor(counted[:].rearrange("p (t e) -> p t e", t=TT), which[:, 0:TT],
                                        which[:, TT:2 * TT], ALU.add).then_inc(counted_ready, 1)
                assert n[0] == BEST_LINKS, n[0]

            @unless_none
            def route_slots(b):
                n = [BEST_LINKS]

                def then(ins, apart=False):
                    n[0] += 1
                    link(ins, tail_chain, b, TAIL_LINKS, n[0], apart)

                then(nc.vector.tensor_tensor(top_sum[:], best[:, :, 0], best[:, :, 1], ALU.add))
                then(nc.vector.tensor_scalar(top_sum[:], top_sum[:], 1e-20, None, ALU.add))
                then(nc.vector.reciprocal(top_sum[:], top_sum[:]))
                nc.vector.tensor_tensor(row[:, :, :, DIM], best[:, :, 0:TOPK],
                                        top_sum[:].unsqueeze(2).to_broadcast([P, TT, TOPK]), ALU.mult)
                then(nc.vector.tensor_copy(row[:].bitcast(I32)[:, :, :, DIM + 1],
                                           token_no[:].unsqueeze(2).to_broadcast([P, TT, TOPK])))
                then(nc.vector.tensor_scalar(token_no[:], token_no[:], float(SEQ), None, ALU.add))
                dve.wait_ge(rank_psum, b.nth(1, 1))
                rank = tail_bank(11)[:, 64:64 + (TT + 1) * EXPERTS].rearrange("p (t e) -> p t e", e=EXPERTS)
                then(nc.vector.tensor_tensor(place[:], rank[:, 0:TT], base[:].unsqueeze(1).to_broadcast(
                    [P, TT, EXPERTS]), ALU.add))
                then(nc.vector.tensor_tensor(base[:], rank[:, TT], base[:], ALU.add))
                for c in range(TOPK):
                    last = nc.vector.tensor_tensor(placed[:, TT * c:TT * c + TT], which[:, TT * c:TT * c + TT],
                                                   place[:], ALU.mult)
                then(last)
                then(nc.vector.tensor_reduce(slotf[:], placed[:], AX, ALU.add))
                nc.vector.tensor_copy(slot[:], slotf[:]).then_inc(slots_ready, 1)
                assert n[0] == TAIL_LINKS, n[0]

            def step(b, prev, nxt, old):
                q_shift(b, 0)
                q_shift(b, 1)
                q_total(b, 0)
                q_shift(b, 2)
                q_total(b, 1)
                route_slots(old)
                context_take(prev, 0)
                context_take(prev, 1)
                q_shift(b, 3)
                q_total(b, 2)
                q_shift(b, 4)
                q_total(b, 3)
                q_shift(b, 5)
                q_total(b, 4)
                q_shift(b, 6)
                q_total(b, 5)
                q_shift(b, 7)
                q_total(b, 6)
                q_total(b, 7)
                k_max(b, 0)
                ln_stats(nxt)
                m_low(prev)
                k_max(b, 1)
                add_attention(prev)
                ln2_stats(prev)
                k_max(b, 2)
                k_max(b, 3)
                ln2_apply(prev)
                k_max(b, 4)
                k_max(b, 5)
                ln_apply(nxt)
                k_max(b, 6)
                k_max(b, 7)
                xt_low(nxt, 0)
                xt_low(nxt, 1)
                route_best(prev)

            steps(dve, step)

        @block.tensor
        def _(pe):
            pe.wait_ge(rw_in, 16)
            for kk in range(KC):
                last = nc.tensor.transpose(bank[0][:, EXPERTS * kk:EXPERTS * kk + EXPERTS], rw[:, P * kk:P * kk + P],
                                           ident[0:EXPERTS, 0:EXPERTS])
            last.then_inc(rw_turned, 1)
            pe.wait_ge(rw_copied, 1)
            pe.wait_ge(consts_pool, 9)

            def first(b):
                return b.is_first(1)

            def qk_free(b, use):
                prev = use - 3
                if prev < 0:
                    if first(b):
                        return
                    pe.wait_ge(k_exp_ready, b.nth(PAIRS, prev + 1))
                elif prev < 2:
                    pe.wait_ge(xt_lo_ready, b.nth(KC, prev + 1))
                elif prev < 2 + Q_UNITS:
                    pe.wait_ge(q_shifted, b.nth(Q_UNITS, prev - 1))
                else:
                    pe.wait_ge(k_exp_ready, b.nth(PAIRS, prev - 9))

            TAIL_READS = [(ctx_ready, 2, 1), (ctx_ready, 2, 2), (g_ready, 4, 1), (g_ready, 4, 2),
                          (g_ready, 4, 3), (g_ready, 4, 4), (m_lo_ready, 1, 1), (res_added, 2, 1),
                          (res_added, 2, 2), (x2t_ready, 2, 1), (x2t_ready, 2, 2), (slots_ready, 1, 1)]

            def tail_free(b, use):
                prev = use - 3
                if prev < 0 and first(b):
                    return
                done, per, n = TAIL_READS[prev % TAIL_USES]
                pe.wait_ge(done, b.nth(per, n if prev >= 0 else n - per))

            @unless_none
            def xt(b, kk):
                pe.wait_ge(xn_ready, b.nth(1, 1))
                qk_free(b, kk)
                for t in range(TT):
                    last = nc.tensor.transpose(qk_bank(kk)[:, P * t:P * t + P], xn[:, t, P * kk:P * kk + P], ident[:])
                last.then_inc(qk_psum, 1)

            def split_product(o, pairs):
                n = 0
                for lh, ll, rh, rl in pairs:
                    for a, c in ((lh, rh), (lh, rl), (ll, rh)):
                        n += 1
                        last = nc.tensor.matmul(o, a, c, start=(n == 1), stop=(n == 3 * len(pairs)))
                return last

            @unless_none
            def q_unit(b, u):
                if u == 0:
                    pe.wait_ge(xt_hi_ready, b.nth(KC, KC))
                    pe.wait_ge(xt_lo_ready, b.nth(KC, KC))
                qk_free(b, 2 + u)
                t, c = P * (u // 2), 512 * (u % 2)
                split_product(qk_bank(2 + u)[:], [
                    (xt_hi[:, b.par, kk, t:t + P], xt_lo[:, b.par, kk, t:t + P],
                     wqk_hi[:, kk, c:c + 512], wqk_lo[:, kk, c:c + 512]) for kk in range(KC)]
                ).then_inc(qk_psum, 1)

            @unless_none
            def k_unit(b, c):
                qk_free(b, 10 + c)
                w = slice(INNER + P * c, INNER + P * c + P)
                split_product(qk_bank(10 + c)[:], [
                    (wqk_hi[:, kk, w], wqk_lo[:, kk, w], xt_hi[:, b.par, kk], xt_lo[:, b.par, kk])
                    for kk in range(KC)]).then_inc(qk_psum, 1)

            @unless_none
            def k_turn(b, c):
                pe.wait_ge(k_exp_ready, b.nth(PAIRS, c + 1))
                if c >= 2 or not first(b):
                    pe.wait_ge(k_ready, b.nth(PAIRS, c - 1))
                for t in range(TT):
                    last = nc.tensor.transpose(k_bank(c)[:, P * t:P * t + P], k_exps[:, c % 2, P * t:P * t + P],
                                               ident[:])
                last.then_inc(k_psum, 1)

            @unless_none
            def context_of(b):
                pe.wait_ge(q_ready, b.nth(Q_UNITS, Q_UNITS))
                pe.wait_ge(k_ready, b.nth(PAIRS, PAIRS))
                for n in range(2):
                    tail_free(b, n)
                    for a in range(4):
                        c = P * (4 * n + a)
                        for t in range(TT):
                            last = nc.tensor.matmul(tail_bank(n)[:, P * a:P * a + P], k[:, t, c:c + P],
                                                    q[:, b.par, t, c:c + P], start=(t == 0), stop=(t == TT - 1))
                    last.then_inc(tail_psum, 1)

            @unless_none
            def g_of(b, n):
                pe.wait_ge(ctx_ready, b.nth(2, n // 2 + 1))
                tail_free(b, 2 + n)
                for a in range(2):
                    last = nc.tensor.matmul(tail_bank(2 + n)[:, DIM * a:DIM * a + DIM], context[:, 2 * n + a],
                                            wo[:, 2 * n + a], start=True, stop=True)
                last.then_inc(tail_psum, 1)

            @unless_none
            def m_of(b):
                pe.wait_ge(g_ready, b.nth(4, 4))
                tail_free(b, 6)
                for kk in range(KC):
                    for a in range(PAIRS):
                        last = nc.tensor.matmul(tail_bank(6)[:, DIM * kk:DIM * kk + DIM],
                                                wv_t[:, a, P * kk:P * kk + P], g[:, a],
                                                start=(a == 0), stop=(a == PAIRS - 1))
                last.then_inc(tail_psum, 1)

            @unless_none
            def attention_of(b):
                pe.wait_ge(m_hi_ready, b.nth(1, 1))
                pe.wait_ge(m_lo_ready, b.nth(1, 1))
                for n in range(2):
                    tail_free(b, 7 + n)
                    for a in range(2):
                        t = P * (2 * n + a)
                        last = split_product(tail_bank(7 + n)[:, DIM * a:DIM * a + DIM], [
                            (xt_hi[:, b.par, kk, t:t + P], xt_lo[:, b.par, kk, t:t + P], m_hi[:, kk], m_lo[:, kk])
                            for kk in range(KC)])
                    last.then_inc(tail_psum, 1)

            @unless_none
            def x2_turn(b):
                pe.wait_ge(row_ready, b.nth(1, 1))
                for kk in range(KC):
                    tail_free(b, 9 + kk)
                    for t in range(TT):
                        last = nc.tensor.transpose(tail_bank(9 + kk)[:, P * t:P * t + P],
                                                   row[:, t, 0, P * kk:P * kk + P], ident[:])
                    last.then_inc(tail_psum, 1)

            @unless_none
            def router(b):
                pe.wait_ge(x2t_ready, b.nth(KC, KC))
                tail_free(b, 11)
                for t in range(TT):
                    for kk in range(KC):
                        last = nc.tensor.matmul(tail_bank(11)[:, EXPERTS * t:EXPERTS * t + EXPERTS],
                                                x2_t[:, kk, P * t:P * t + P], rw_t[:, kk],
                                                start=(kk == 0), stop=(kk == KC - 1))
                last.then_inc(tail_psum, 1)

            @unless_none
            def ranks(b):
                pe.wait_ge(counted_ready, b.nth(1, 1))
                for t in range(TT + 1):
                    o = tail_bank(11)[:, 64 + EXPERTS * t:64 + EXPERTS * t + EXPERTS]
                    terms = [(every, s) for s in range(t)] + [(before, t)] * (t < TT)
                    for n, (a, s) in enumerate(terms):
                        last = nc.tensor.matmul(o, a[:], counted[:, EXPERTS * s:EXPERTS * s + EXPERTS],
                                                start=(n == 0), stop=(n == len(terms) - 1))
                last.then_inc(rank_psum, 1)

            def step(b, prev, nxt, old):
                q_unit(b, 0)
                q_unit(b, 1)
                q_unit(b, 2)
                ranks(old)
                context_of(prev)
                q_unit(b, 3)
                q_unit(b, 4)
                q_unit(b, 5)
                g_of(prev, 0)
                g_of(prev, 1)
                q_unit(b, 6)
                g_of(prev, 2)
                g_of(prev, 3)
                q_unit(b, 7)
                k_unit(b, 0)
                m_of(prev)
                k_unit(b, 1)
                k_turn(b, 0)
                attention_of(prev)
                k_unit(b, 2)
                k_turn(b, 1)
                k_unit(b, 3)
                k_unit(b, 4)
                k_turn(b, 2)
                k_unit(b, 5)
                k_turn(b, 3)
                x2_turn(prev)
                k_unit(b, 6)
                k_turn(b, 4)
                k_unit(b, 7)
                k_turn(b, 5)
                xt(nxt, 0)
                xt(nxt, 1)
                router(prev)
                k_turn(b, 6)
                k_turn(b, 7)

            steps(pe, step)


def experts(nc, ctx, sem, bank, ident, base, base0, w1, w2, queue_d, out):
    def sbuf(name, shape, dt=F32):
        return ctx.enter_context(nc.sbuf_tensor(name, shape, dt))

    w1_hi = sbuf("w1_hi", [P, KC, EXPERTS * MAXW], F32R)
    w1_lo = sbuf("w1_lo", [P, KC, EXPERTS * MAXW], F32R)
    w2_hi = sbuf("w2_hi", [P, EXPERTS * FC, DIM], F32R)
    w2_lo = sbuf("w2_lo", [P, EXPERTS * FC, DIM], F32R)
    raw = sbuf("raw", [P, 2, TOTAL_W])
    rows = sbuf("queue_rows", [P, SLOTS, ROW])
    x_hi = sbuf("x_hi", [P, 2, DIM], F32R)
    x_lo = sbuf("x_lo", [P, 2, DIM], F32R)
    relu = sbuf("relu", [P, 2, MAXW])
    act_w = sbuf("act_w", [P, 2, MAXW])
    a_hi = sbuf("a_hi", [P, 2, MAXW], F32R)
    a_lo = sbuf("a_lo", [P, 2, MAXW], F32R)
    y = sbuf("y", [P, 2, DIM])
    filler = sbuf("filler", [P, ROW])
    count = sbuf("count", [P, EXPERTS])
    count_i = sbuf("count_i", [P, EXPERTS], I32)
    tiles = sbuf("tiles", [P, EXPERTS])
    upto = sbuf("upto", [P, EXPERTS, EXPERTS])
    upto_tiles = sbuf("upto_tiles", [P, EXPERTS, EXPERTS])
    end = sbuf("end", [P, EXPERTS])
    end_i = sbuf("end_i", [P, EXPERTS], I32)
    tile_no = sbuf("tile_no", [1, TABLE])
    passed = sbuf("passed", [1, TABLE, EXPERTS])
    passed_tiles = sbuf("passed_tiles", [1, TABLE, EXPERTS])
    expert_f = sbuf("expert_f", [1, TABLE])
    start_f = sbuf("start_f", [1, TABLE])
    expert_of = sbuf("expert_of", [1, TABLE], I32)
    row_of = sbuf("row_of", [1, TABLE], I32)
    differs = sbuf("differs", [1, TABLE])
    no_rows = sbuf("no_rows", [1, TABLE])
    apart = sbuf("apart", [1, TABLE], I32)

    raw_in = [sem(f"raw_in{i}") for i in range(2)]
    rows_in = [sem(f"rows_in{i}") for i in range(SLOTS)]
    consts3, filler_ready, pads_zero, ends_ready, filled, table_chain, table_ready = (sem(n) for n in (
        "consts3", "filler_ready", "pads_zero", "ends_ready", "filled", "table_chain", "table_ready"))
    w_hi_ready, w_lo_ready, x_turned, x_hi_ready, x_lo_ready, up_done, relu_ready, act_ready = (sem(n) for n in (
        "w_hi_ready", "w_lo_ready", "x_turned", "x_hi_ready", "x_lo_ready", "up_done", "relu_ready", "act_ready"))
    act_turned, a_hi_ready, a_lo_ready, down_done, y_ready, pool_passed3 = (sem(n) for n in (
        "act_turned", "a_hi_ready", "a_lo_ready", "down_done", "y_ready", "pool_passed3"))
    halves_zero = sem("halves_zero")
    added = [sem(f"added{i}") for i in range(2)]

    narrow = sum(w for w in WIDTHS if w < MAXW)
    w1_v = w1.rearrange("(k p) n -> k p n", p=P)
    w2_v = w2.rearrange("(h c p) n -> h p c n", p=P, h=2)

    def piece(n, store1, store2):
        r = raw[:, n % 2]
        if n < KC:
            s = store1[:, n]
            return [(r[:, 0:narrow].rearrange("p (e w) -> p e w", w=256),
                     s[:, 0:NARROW * MAXW].rearrange("p (e w) -> p e w", w=MAXW)[:, :, 0:256]),
                    (r[:, narrow:], s[:, NARROW * MAXW:])]
        r = r.rearrange("p (c n) -> p c n", n=DIM)
        if n == KC:
            return [(r[:, 0:8].rearrange("p (e c) n -> p e (c n)", c=2),
                     store2[:, 0:NARROW * FC].rearrange("p (e c) n -> p e (c n)", c=FC)[:, :, 0:2 * DIM]),
                    (r[:, 8:12], store2[:, NARROW * FC:NARROW * FC + 4])]
        return [(r, store2[:, NARROW * FC + 4:])]

    def need(engine, s, value):
        if not isinstance(value, int) or value > 0:
            engine.wait_ge(s, value)

    def all_turns(engine, step):
        def of_turn(turn):
            last = engine.value_load(expert_of[0:1, bass.ds(turn * SLOTS + SLOTS - 1, 1)], min_val=0,
                                     max_val=EXPERTS - 1)
            with engine.If(last < NARROW):
                for u in range(SLOTS):
                    step(turn, u, NARROW_W)
            with engine.Else():
                for u in range(SLOTS):
                    step(turn, u, MAXW)

        of_turn(0)
        with engine.Fori(1, TILES // SLOTS) as i:
            of_turn(i)

    with nc.Block() as block:
        @block.sync
        def _(sp):
            for n in range(4):
                if n >= 2:
                    sp.wait_ge(w_lo_ready, n - 1)
                dst = raw[:, n % 2] if n < KC else raw[:, n % 2].rearrange("p (c n) -> p c n", n=DIM)
                sp.dma_start(dst, w1_v[n] if n < KC else w2_v[n - KC]).then_inc(raw_in[n % 2], 16)
            sp.wait_ge(filler_ready, 1)
            sp.dma_start(out[TOKENS:TOKENS + P, :], filler[:, 0:DIM]).then_inc(filled, 16)
            sp.dma_start(queue_d[FILLER_ROW:FILLER_ROW + P, :], filler[:]).then_inc(filled, 16)
            sp.wait_ge(ends_ready, 1)
            for e in range(EXPERTS):
                at = sp.value_load(end_i[0:1, e:e + 1], min_val=0, max_val=FILLER_ROW)
                sp.dma_start(queue_d[bass.ds(at, P), :], filler[:]).then_inc(filled, 16)
            sp.wait_ge(table_ready, 1)
            sp.wait_ge(filled, 16 * (EXPERTS + 2))

            def load(j, u, turn):
                at = sp.value_load(row_of[0:1, bass.ds(j, 1)], min_val=0, max_val=FILLER_ROW)
                if turn is not None:
                    sp.wait_ge(added[u % 2], (turn * (SLOTS // 2) + u // 2 + 1) * 16)
                sp.dma_start(rows[:, u], queue_d[bass.ds(at, P), :]).then_inc(rows_in[u], 16)

            for j in range(SLOTS):
                load(j, j, None)
            with sp.Fori(1, TILES // SLOTS) as i:
                for u in range(SLOTS):
                    load(i * SLOTS + u, u, i - 1)
            for u in range(AHEAD):
                load(TILES + u, u, TILES // SLOTS - 1)

        @block.gpsimd
        def _(pool):
            nc.gpsimd.memset(filler[:], 0.0).then_inc(consts3, 1)
            nc.gpsimd.memset(upto[:], 1.0).then_inc(consts3, 1)
            nc.gpsimd.iota(tile_no[:], [[1, TABLE]], base=0, channel_multiplier=0,
                           allow_small_or_imprecise_dtypes=True).then_inc(consts3, 1)
            pool.wait_ge(consts3, 3)
            nc.gpsimd.affine_select(out=upto[:], in_=upto[:], compare_op=ALU.is_ge, fill=0.0, base=0,
                                    pattern=[[1, EXPERTS], [-1, EXPERTS]], channel_multiplier=0).then_inc(consts3, 1)
            nc.gpsimd.iota(filler[:].bitcast(I32)[:, DIM + 1:ROW], [[1, 1]], base=TOKENS, channel_multiplier=1
                           ).then_inc(filler_ready, 1)
            for w in (w1_hi, w1_lo):
                for k in range(KC):
                    pad = w[:, k].bitcast(F32)[:, 0:NARROW * MAXW].rearrange("p (e w) -> p e w", w=MAXW)
                    nc.gpsimd.memset(pad[:, :, 256:MAXW], 0.0).then_inc(pads_zero, 1)
            for w in (w2_hi, w2_lo):
                pad = w[:].bitcast(F32)[:, 0:NARROW * FC].rearrange("p (e c) n -> p e (c n)", c=FC)
                nc.gpsimd.memset(pad[:, :, 2 * DIM:], 0.0).then_inc(pads_zero, 1)

            def add(j, u, pair):
                wait_apart(pool, y_ready, j + 1, pool_passed3)
                if not isinstance(j, int) or j >= 2:
                    wait_apart(pool, added[u % 2], pair * 16, pool_passed3)
                if isinstance(j, int) and 1 <= j <= 2:
                    wait_apart(pool, added[1 - u % 2], 16, pool_passed3)
                elif not isinstance(j, int) or j > 2:
                    differs16 = pool.value_load(apart[0:1, bass.ds(j, 1)], min_val=0, max_val=16)
                    wait_apart(pool, added[1 - u % 2], (pair + u % 2 - 1) * 16 + differs16, pool_passed3)
                pool.indirect_dma_start(
                    out=out, in_=y[:, u % 2, :], in_offset=None, compute_op=ALU.add,
                    out_offset=bass.IndirectOffsetOnAxis(ap=rows[:, u, DIM + 1:ROW].bitcast(U32), axis=0)
                ).then_inc(added[u % 2], 16)

            pool.wait_ge(table_ready, 1)
            for j in range(SLOTS):
                add(j, j, j // 2)
            with pool.Fori(1, TILES // SLOTS) as i:
                for u in range(SLOTS):
                    add(i * SLOTS + u, u, i * (SLOTS // 2) + u // 2)
            for s in added:
                pool.wait_ge(s, 16 * TILES // 2)

        @block.scalar
        def _(act):
            for n in range(4):
                act.wait_ge(raw_in[n % 2], 16 * (n // 2 + 1))
                for src, dst in piece(n, w1_hi, w2_hi):
                    last = nc.scalar.activation(dst, src, ACT.Copy)
                last.then_inc(w_hi_ready, 1)

            def x_high(j, u):
                need(act, x_turned, j + 1)
                need(act, up_done, j - 1)
                nc.scalar.activation(x_hi[:, u % 2], bank[u % 2][:, 0:DIM], ACT.Copy).then_inc(x_hi_ready, 1)

            def take_relu(j, u, width):
                need(act, up_done, j + 1)
                need(act, act_ready, j - 1)
                nc.scalar.activation(relu[:, u % 2, 0:width], bank[2 + u % 2][:, 0:width], ACT.Relu
                                     ).then_inc(relu_ready, 1)

            def act_high(j, u, width):
                need(act, act_turned, j + 1)
                need(act, down_done, j - 1)
                nc.scalar.activation(a_hi[:, u % 2, 0:width], bank[4 + u % 2][:, 0:width], ACT.Copy
                                     ).then_inc(a_hi_ready, 1)

            def take_y(j, u, pair):
                need(act, down_done, j + 1)
                need(act, added[u % 2], pair * 16)
                nc.scalar.activation(y[:, u % 2], bank[6 + u % 2][:, 0:DIM], ACT.Copy).then_inc(y_ready, 1)

            def step(turn, u, width):
                j, pair = turn * SLOTS + u, turn * (SLOTS // 2) + u // 2
                take_relu(j, u, width)
                x_high(j + AHEAD, u)
                if not isinstance(j, int) or j >= 1:
                    act_high(j - 1, u + 1, width)
                if not isinstance(j, int) or j >= 2:
                    take_y(j - 2, u, pair - 1)

            x_high(0, 0)
            x_high(1, 1)
            act.wait_ge(table_ready, 1)
            all_turns(act, step)
            act_high(TILES - 1, 1, MAXW)
            take_y(TILES - 2, 0, TILES // 2 - 1)
            take_y(TILES - 1, 1, TILES // 2 - 1)

        @block.vector
        def _(dve):
            n = [0]

            def link(ins):
                n[0] += 1
                ins.then_inc(table_chain, 1)
                dve.wait_ge(table_chain, n[0])

            for a in (act_w[:], a_hi[:].bitcast(F32), a_lo[:].bitcast(F32)):
                nc.vector.memset(a[:, :, NARROW_W:MAXW], 0.0).then_inc(halves_zero, 1)
            link(nc.vector.tensor_copy(end_i[:], base[:]))
            link(nc.vector.tensor_tensor(count[:], base[:], base0[:], ALU.subtract))
            link(nc.vector.tensor_scalar(count[:], count[:], float(P - 1), None, ALU.add))
            link(nc.vector.tensor_copy(count_i[:], count[:]))
            nc.vector.tensor_scalar(count_i[:], count_i[:], 7, None, ALU.logical_shift_right).then_inc(ends_ready, 1)
            dve.wait_ge(ends_ready, 1)
            link(nc.vector.tensor_copy(tiles[:], count_i[:]))
            dve.wait_ge(consts3, 4)
            link(nc.vector.tensor_tensor(upto_tiles[:], upto[:], tiles[:].unsqueeze(1).to_broadcast(
                [P, EXPERTS, EXPERTS]), ALU.mult))
            link(nc.vector.tensor_reduce(end[:], upto_tiles[:], AX, ALU.add))
            full = [1, TABLE, EXPERTS]
            link(nc.vector.tensor_tensor(passed[:], end[0:1].unsqueeze(1).to_broadcast(full),
                                         tile_no[:].unsqueeze(2).to_broadcast(full), ALU.is_le))
            link(nc.vector.tensor_tensor(passed_tiles[:], passed[:], tiles[0:1].unsqueeze(1).to_broadcast(full),
                                         ALU.mult))
            nc.vector.tensor_reduce(expert_f[:], passed[:], AX, ALU.add)
            link(nc.vector.tensor_reduce(start_f[:], passed_tiles[:], AX, ALU.add))
            link(nc.vector.tensor_tensor(start_f[:], tile_no[:], start_f[:], ALU.subtract))
            link(nc.vector.tensor_scalar(start_f[:], start_f[:], float(P), None, ALU.mult))
            link(nc.vector.scalar_tensor_tensor(out=start_f[:], in0=expert_f[:], scalar=float(QROWS), in1=start_f[:],
                                                op0=ALU.mult, op1=ALU.add))
            link(nc.vector.tensor_scalar(row_of[:], start_f[:], float(FILLER_ROW), None, ALU.min))
            link(nc.vector.tensor_scalar(no_rows[:], expert_f[:], float(EXPERTS), None, ALU.is_ge))
            link(nc.vector.tensor_copy(differs[:], no_rows[:]))
            link(nc.vector.tensor_tensor(differs[:, 1:], expert_f[:, 1:], expert_f[:, 0:TABLE - 1], ALU.not_equal))
            link(nc.vector.tensor_tensor(differs[:], differs[:], no_rows[:], ALU.max))
            link(nc.vector.tensor_scalar(apart[:], differs[:], 16.0, None, ALU.mult))
            nc.vector.tensor_scalar(expert_of[:], expert_f[:], float(EXPERTS - 1), None, ALU.min
                                    ).then_inc(table_ready, 1)
            for m in range(4):
                dve.wait_ge(w_hi_ready, m + 1)
                for (src, dst), (_, hi) in zip(piece(m, w1_lo, w2_lo), piece(m, w1_hi, w2_hi)):
                    last = nc.vector.tensor_tensor(dst, src, hi.bitcast(F32), ALU.subtract)
                last.then_inc(w_lo_ready, 1)

            def x_low(j, u):
                need(dve, x_hi_ready, j + 1)
                nc.vector.tensor_tensor(x_lo[:, u % 2], bank[u % 2][:, 0:DIM], x_hi[:, u % 2].bitcast(F32),
                                        ALU.subtract).then_inc(x_lo_ready, 1)

            def square(j, u, width):
                need(dve, relu_ready, j + 1)
                need(dve, act_turned, j - 1)
                nc.vector.scalar_tensor_tensor(out=act_w[:, u % 2, 0:width], in0=relu[:, u % 2, 0:width],
                                               scalar=rows[:, u, DIM:DIM + 1], in1=relu[:, u % 2, 0:width],
                                               op0=ALU.mult, op1=ALU.mult).then_inc(act_ready, 1)

            def act_low(j, u, width):
                need(dve, a_hi_ready, j + 1)
                nc.vector.tensor_tensor(a_lo[:, u % 2, 0:width], bank[4 + u % 2][:, 0:width],
                                        a_hi[:, u % 2, 0:width].bitcast(F32), ALU.subtract).then_inc(a_lo_ready, 1)

            def step(turn, u, width):
                j = turn * SLOTS + u
                square(j, u, width)
                x_low(j + AHEAD, u)
                if not isinstance(j, int) or j >= 1:
                    act_low(j - 1, u + 1, width)

            x_low(0, 0)
            x_low(1, 1)
            dve.wait_ge(table_ready, 1)
            all_turns(dve, step)
            act_low(TILES - 1, 1, MAXW)

        @block.tensor
        def _(pe):
            def x_turn(j, u, slot, turn):
                need(pe, rows_in[slot], (turn + 1) * 16)
                need(pe, x_lo_ready, j - 1)
                for k in range(KC):
                    last = nc.tensor.transpose(bank[u % 2][:, P * k:P * k + P], rows[:, slot, P * k:P * k + P],
                                               ident[:])
                last.then_inc(x_turned, 1)

            def split_product(o, pairs, parts):
                n = 0
                for lh, ll, rh, rl in pairs:
                    for a, c in ((lh, rh), (lh, rl), (ll, rh)):
                        n += 1
                        last = nc.tensor.matmul(o, a, c, start=(n == 1), stop=(n == parts))
                return last

            def up(j, u, e, width):
                need(pe, x_lo_ready, j + 1)
                need(pe, act_ready, j - 1)
                w = bass.ds(e * MAXW, width)
                split_product(bank[2 + u % 2][:, 0:width], [
                    (x_hi[:, u % 2, P * k:P * k + P], x_lo[:, u % 2, P * k:P * k + P], w1_hi[:, k, w], w1_lo[:, k, w])
                    for k in range(KC)], 3 * KC).then_inc(up_done, 1)

            def act_turn(j, u, width):
                need(pe, act_ready, j + 1)
                need(pe, a_lo_ready, j - 1)
                for f in range(width // P):
                    last = nc.tensor.transpose(bank[4 + u % 2][:, P * f:P * f + P], act_w[:, u % 2, P * f:P * f + P],
                                               ident[:])
                last.then_inc(act_turned, 1)

            def down(j, u, e, width):
                chunks = width // P
                need(pe, a_lo_ready, j + 1)
                need(pe, y_ready, j - 1)
                hi, lo = (w[:].rearrange("p c n -> p (c n)") for w in (w2_hi, w2_lo))
                at = [bass.ds(e * (FC * DIM) + f * DIM, DIM) for f in range(chunks)]
                split_product(bank[6 + u % 2][:, 0:DIM], [
                    (a_hi[:, u % 2, P * f:P * f + P], a_lo[:, u % 2, P * f:P * f + P], hi[:, at[f]], lo[:, at[f]])
                    for f in range(chunks)], 3 * chunks).then_inc(down_done, 1)

            def load_expert(j):
                return pe.value_load(expert_of[0:1, bass.ds(j, 1)], min_val=0, max_val=EXPERTS - 1)

            def step(turn, u, width):
                j = turn * SLOTS + u
                if u == 0:
                    e[0] = load_expert(j)
                up(j, u, e[u], width)
                if u + 1 < SLOTS:
                    e[u + 1] = load_expert(j + 1)
                x_turn(j + AHEAD, u, (u + AHEAD) % SLOTS, turn + (u + AHEAD) // SLOTS)
                if not isinstance(j, int) or j >= 1:
                    act_turn(j - 1, u + 1, width)
                if not isinstance(j, int) or j >= 2:
                    down(j - 2, u, e[u - 2] if u >= 2 else load_expert(j - 2), width)

            e = {}
            x_turn(0, 0, 0, 0)
            x_turn(1, 1, 1, 0)
            pe.wait_ge(table_ready, 1)
            pe.wait_ge(w_lo_ready, 4)
            pe.wait_ge(pads_zero, 6)
            pe.wait_ge(halves_zero, 3)
            all_turns(pe, step)
            act_turn(TILES - 1, 1, MAXW)
            for u in range(2):
                down(TILES - 2 + u, u, load_expert(TILES - 2 + u), MAXW)


_INS = ['x', 'L0_tok_embed_table', 'L0_tok_conv_w', 'L0_tok_conv_b', 'L0_attn_w_qkv', 'L0_attn_w_out',
        'L0_attn_b_out', 'L0_ffn_router_w', 'L0_ffn_w1', 'L0_ffn_w2']


def kernel(**inputs):
    import numpy as np
    import concourse.bacc as bacc
    from concourse.bass_utils import run_bass_kernel_spmd

    nc = bacc.Bacc("TRN2", target_bir_lowering=False, num_devices=1)
    arrays, args = {}, []
    for name in _INS:
        a = np.ascontiguousarray(inputs[name])
        if name == "x":
            a = np.concatenate([a[:, SEQ - PAD:], a[:, :SEQ - PAD]], axis=1)
            a = np.ascontiguousarray(a.reshape(BATCHES, NBLK, BLK).transpose(1, 0, 2).reshape(P, BLK))
        arrays[f"in_{name}"] = a
        args.append(nc.dram_tensor(f"in_{name}", a.shape, mybir.dt.from_np(a.dtype), kind="ExternalInput").ap())
    out = nc.dram_tensor("out", (TOKENS + P, DIM), F32, kind="ExternalOutput").ap()
    tower(nc, *args, out)
    r = run_bass_kernel_spmd(nc, [arrays], core_ids=[0])
    return r.results[0]["out"][:TOKENS].reshape(BATCHES, SEQ, DIM)
```

```python
from contextlib import ExitStack

import concourse.bass as bass
from concourse import mybir

F32 = mybir.dt.float32
F32R = mybir.dt.float32r
BF16 = mybir.dt.bfloat16
I32 = mybir.dt.int32
U32 = mybir.dt.uint32
ALU = mybir.AluOpType
ACT = mybir.ActivationFunctionType
AX = mybir.AxisListType.X

P = 128
BATCHES, SEQ, DIM = 8, 512, 256
TOKENS = BATCHES * SEQ
TAPS = 31
PAD = TAPS // 2
HEADS, DH = 16, 64
INNER = HEADS * DH
SCALE = DH ** -0.5
EPS = 1e-5

BLK = 32
CG = P // BLK
NBLK = SEQ // BLK
GROUPS = DIM // CG
SETS = GROUPS // 4
WIN = 2 * BLK
WPAD = 96

KC = DIM // P
TT = SEQ // P
PAIRS = INNER // P
COLS = P // TT

EXPERTS = 8
NARROW_W, MAXW = 256, 512
WIDTHS = [NARROW_W] * 4 + [MAXW] * 4
NARROW = sum(w == NARROW_W for w in WIDTHS)
FC = MAXW // P
TOPK = 2
QROWS = TOKENS + P
FILLER_ROW = EXPERTS * QROWS
ROW = DIM + 2
TILES = 72
AHEAD = 2
TABLE = TILES + AHEAD
SLOTS = 8
TOTAL_W = sum(WIDTHS)


class Batch:

    def __init__(self, n, par, half):
        self.n, self.par, self.half = n, par, half

    def nth(self, per, k):
        return self.n * per + k

    def is_first(self, count):
        return isinstance(self.n, int) and self.n < count


class Dispatch:

    def __init__(self, sbuf, sem):
        self.filler = sbuf("filler", [P, ROW])
        self.count = sbuf("count", [P, EXPERTS])
        self.count_i = sbuf("count_i", [P, EXPERTS], I32)
        self.tiles = sbuf("tiles", [P, EXPERTS])
        self.upto = sbuf("upto", [P, EXPERTS, EXPERTS])
        self.end = sbuf("end", [P, EXPERTS])
        self.end_i = sbuf("end_i", [P, EXPERTS], I32)
        self.tile_no = sbuf("tile_no", [1, TABLE])
        self.expert_of = sbuf("expert_of", [1, TABLE], I32)
        self.row_of = sbuf("row_of", [1, TABLE], I32)
        self.apart = sbuf("apart", [1, TABLE], I32)
        self.consts, self.filler_ready, self.ends_ready, self.filled, self.chain, self.ready = (sem(n) for n in (
            "table_consts", "filler_ready", "ends_ready", "filled", "table_chain", "table_ready"))


def wait_apart(engine, sem, value, passed):
    engine.wait_ge(sem, value)
    engine.sem_inc(passed, 1)


def unless_none(fn):
    def part(b, *args):
        if b is not None:
            fn(b, *args)
    return part


def on_all(vector):
    return vector.partition_broadcast(P)


def tower(nc, x, embeddings, conv_w, conv_b, w_qkv, w_out, b_out, router_w, w1, w2, out):
    top = ExitStack()
    with top:
        bank = [top.enter_context(nc.psum_tensor(f"bank{i}", [P, 512], F32)) for i in range(8)]

        def sem(name):
            return top.enter_context(nc.semaphore(name))

        def sbuf(stack, name, shape, dt=F32):
            return stack.enter_context(nc.sbuf_tensor(name, shape, dt))

        taps_d = nc.dram_tensor("taps_d", [DIM, WPAD], F32).ap()
        h_d = nc.dram_tensor("h_d", [TOKENS, DIM], F32).ap()
        queue_d = nc.dram_tensor("queue_d", [FILLER_ROW + P, ROW], F32).ap()

        ident = sbuf(top, "ident", [P, P])
        base = sbuf(top, "base", [P, EXPERTS])
        base0 = sbuf(top, "base0", [P, EXPERTS])
        store = sbuf(top, "store", [P, 3, TOTAL_W])
        table = Dispatch(lambda *args: sbuf(top, *args), sem)
        w1_first = sbuf(top, "w1_first", [P, 2, EXPERTS * MAXW], F32R)
        wqk_hi, wqk_lo = (w1_first[:, n].rearrange("p (k n) -> p k n", k=KC) for n in range(2))
        with ExitStack() as early:
            second_half = sbuf(early, "second_half", [P, 2 * EXPERTS * MAXW])[:]
        w1_second = sbuf(top, "w1_second", [P, 2, EXPERTS * MAXW], F32R)
        w1_parts = (w1_first, w1_second)
        w1_hi_ready, w1_lo_ready, w1_zero = (sem(n) for n in ("w1_hi_ready", "w1_lo_ready", "w1_zero"))
        h_stored = [sem(f"h_stored{n}") for n in range(3)]
        raw_in = [sem(f"raw_in{n}") for n in range(4)]

        with ExitStack() as attn_ctx:
            wv_t = sbuf(attn_ctx, "wv_t", [P, PAIRS, DIM])
            wo = sbuf(attn_ctx, "wo", [P, PAIRS, DIM])
            bo_all = sbuf(attn_ctx, "bo_all", [P, DIM])
            with ExitStack() as conv_ctx:
                convolve(nc, conv_ctx, sem, bank, ident, x, embeddings, conv_w, conv_b, w_qkv, w_out, b_out,
                         taps_d, h_d, store, h_stored, second_half, wqk_hi, wqk_lo, wv_t, wo, bo_all)
            with ExitStack() as ctx:
                attend(nc, ctx, sem, bank, ident, base, base0, router_w, w1, w2, h_d, store, h_stored, raw_in,
                       table, queue_d, out, second_half, wqk_hi, wqk_lo, wv_t, wo, bo_all,
                       w1_parts, w1_hi_ready, w1_lo_ready, w1_zero)
        with ExitStack() as ctx:
            experts(nc, ctx, sem, bank, ident, store, raw_in, table, queue_d, out, w1_parts, w1_lo_ready, w1_zero)


def convolve(nc, ctx, sem, bank, ident, x, embeddings, conv_w, conv_b, w_qkv, w_out, b_out,
             taps_d, h_d, store, h_stored, second_half, wqk_hi, wqk_lo, wv_t, wo, bo_all):
    def sbuf(name, shape, dt=F32):
        return ctx.enter_context(nc.sbuf_tensor(name, shape, dt))

    ids = sbuf("ids", [P, BLK], I32)
    rows = second_half.rearrange("p (i c) -> p i c", c=DIM)
    turned = sbuf("turned", [P, 4, 4, NBLK + 1, BATCHES])
    taps = sbuf("taps", [P, KC, TAPS])
    padded = sbuf("padded", [P, KC, WPAD])
    windows = sbuf("windows", [P, GROUPS, WIN])
    banded = sbuf("banded", [P, 2, 16, WIN, CG])
    same_ch = sbuf("same_ch", [P, CG])
    head_rows = sbuf("head_rows", [P, 1])
    tail_rows = sbuf("tail_rows", [P, 1])
    cb_all = sbuf("cb_all", [P, DIM])
    h = store[:].rearrange("p a n -> p (a n)")[:, 0:BLK * DIM].rearrange("p (o c) -> p o c", c=DIM)
    wqk = sbuf("wqk", [P, KC, 2 * INNER])
    wv = sbuf("wv", [P, KC, INNER])

    ids_in, taps_in, bias_in, wqk_in, wv_in, wo_in = (sem(n) for n in (
        "ids_in", "taps_in", "bias_in", "wqk_in", "wv_in", "wo_in"))
    taps_out, windows_sp, windows_act, gathered = (sem(n) for n in (
        "taps_out", "windows_sp", "windows_act", "gathered"))
    padded_zero, padded_ready, ident_zero, ident_ready, masks_ready = (sem(n) for n in (
        "padded_zero", "padded_ready", "ident_zero", "ident_ready", "masks_ready"))
    rows_turned, turned_ready, banded_ready, conv_done, conv_added = (sem(n) for n in (
        "rows_turned", "turned_ready", "banded_ready", "conv_done", "conv_added"))
    wqk_hi_ready, wqk_lo_ready, wv_turned, wv_copied = (sem(n) for n in (
        "wqk_hi_ready", "wqk_lo_ready", "wv_turned", "wv_copied"))

    taps_v = taps_d.rearrange("(c g) j -> c g j", c=CG)

    def load_window(eng, i, done):
        return eng.dma_start(windows[CG * i:CG * i + CG, :, :],
                             taps_v[:, :, 31 - i:31 - i + WIN]).then_inc(done, 16)

    with nc.Block() as block:
        @block.sync
        def _(sp):
            sp.dma_start(ids[:], x).then_inc(ids_in, 16)
            sp.dma_start(taps[:], conv_w.rearrange("(p a) o k -> p a (o k)", a=KC)).then_inc(taps_in, 16)
            sp.wait_ge(padded_ready, 1)
            sp.dma_start(taps_d.rearrange("(p a) j -> p a j", a=KC), padded[:]).then_inc(taps_out, 16)
            sp.wait_ge(taps_out, 16)
            for i in range(0, BLK, 2):
                load_window(sp, i, windows_sp)
            sp.dma_start(wv[:], w_qkv.rearrange("(k p) n -> p k n", p=P)[:, :, 2 * INNER:3 * INNER]
                         ).then_inc(wv_in, 16)
            sp.dma_start(cb_all[:], on_all(conv_b)).then_inc(bias_in, 16)
            sp.wait_ge(gathered, 16 * BLK)
            sp.dma_start(wqk[:], w_qkv.rearrange("(k p) n -> p k n", p=P)[:, :, 0:2 * INNER]).then_inc(wqk_in, 16)
            sp.dma_start(wo[:], w_out.rearrange("(a p) n -> p a n", p=P)).then_inc(wo_in, 16)
            sp.dma_start(bo_all[:], on_all(b_out)).then_inc(wo_in, 16)
            sp.wait_ge(wo_in, 32)
            sp.wait_ge(conv_added, SETS)
            for b in range(2):
                store_h(sp, h_d, store, b).then_inc(h_stored[b], 16)

        @block.gpsimd
        def _(pool):
            nc.gpsimd.memset(ident[:], 0.0).then_inc(ident_zero, 1)
            pool.wait_ge(ident_zero, 1)
            nc.gpsimd.affine_select(out=ident[:], in_=ident[:], compare_op=ALU.not_equal, fill=1.0, base=0,
                                    pattern=[[-1, P]], channel_multiplier=1).then_inc(ident_ready, 1)
            pool.wait_ge(ids_in, 16)
            for i in range(BLK):
                pool.indirect_dma_start(out=rows[:, i, :], out_offset=None, in_=embeddings,
                                        in_offset=bass.IndirectOffsetOnAxis(ap=ids[:, i:i + 1].bitcast(U32), axis=0)
                                        ).then_inc(gathered, 16)
            for k in range(KC):
                pool.wait_ge(wqk_hi_ready, k + 1)
                nc.gpsimd.tensor_tensor(wqk_lo[:, k], wqk[:, k], wqk_hi[:, k].bitcast(F32), ALU.subtract
                                        ).then_inc(wqk_lo_ready, 1)

        @block.scalar
        def _(act):
            act.wait_ge(taps_out, 16)
            for i in range(1, BLK, 2):
                load_window(act, i, windows_act)

            def make_banded(q):
                if q >= 2:
                    act.wait_ge(conv_done, 4 * (q - 1))
                for c in range(CG):
                    last = nc.scalar.activation(banded[:, q % 2, :, :, c], windows[:, 16 * q:16 * q + 16, :],
                                                ACT.Copy, scale=same_ch[:, c:c + 1])
                last.then_inc(banded_ready, 1)

            act.wait_ge(windows_sp, 16 * (BLK // 2))
            act.wait_ge(windows_act, 16 * (BLK // 2))
            act.wait_ge(masks_ready, 3)
            make_banded(0)
            make_banded(1)
            act.wait_ge(wqk_in, 16)
            for k in range(KC):
                nc.scalar.activation(wqk_hi[:, k], wqk[:, k], ACT.Copy).then_inc(wqk_hi_ready, 1)
            make_banded(2)
            make_banded(3)

        @block.vector
        def _(dve):
            nc.vector.memset(padded[:], 0.0).then_inc(padded_zero, 1)
            dve.wait_ge(padded_zero, 1)
            dve.wait_ge(taps_in, 16)
            nc.vector.tensor_copy(padded[:, :, 33:33 + TAPS], taps[:, :, ::-1]).then_inc(padded_ready, 1)
            dve.wait_ge(ident_ready, 1)
            nc.vector.tensor_reduce(same_ch[:], ident[:].rearrange("p (i c) -> p c i", c=CG), AX, ALU.add
                                    ).then_inc(masks_ready, 1)
            nc.vector.tensor_reduce(tail_rows[:], ident[:, 0:CG * PAD], AX, ALU.add).then_inc(masks_ready, 1)
            nc.vector.tensor_reduce(head_rows[:], ident[:, CG * PAD:P], AX, ALU.add).then_inc(masks_ready, 1)
            dve.wait_ge(masks_ready, 3)

            def take_turned(s):
                dve.wait_ge(rows_turned, s + 1)
                src = bank[s % 4][:].rearrange("p (g s b) -> p g s b", g=4, s=NBLK)
                dst = turned[:, s % 4]
                nc.vector.tensor_copy(dst[:, :, 1:NBLK], src[:, :, 1:NBLK])
                nc.vector.tensor_scalar(dst[:, :, 0], src[:, :, 0], head_rows[:, 0:1], None, ALU.mult)
                nc.vector.tensor_scalar(dst[:, :, NBLK], src[:, :, 0], tail_rows[:, 0:1], None, ALU.mult
                                        ).then_inc(turned_ready, 1)

            def add_bias(s):
                dve.wait_ge(conv_done, s + 1)
                if s == 0:
                    dve.wait_ge(bias_in, 16)
                src = bank[4 + s % 4][:].rearrange("p (g o c) -> p g o c", g=4, c=CG)
                dst = h[:].rearrange("p o (c g) -> p g o c", c=CG)[:, 4 * s:4 * s + 4]
                bias = cb_all[:].rearrange("p (c g) -> p g c", c=CG)[:, 4 * s:4 * s + 4].unsqueeze(2
                    ).to_broadcast([P, 4, BLK, CG])
                nc.vector.tensor_tensor(dst, src, bias, ALU.add).then_inc(conv_added, 1)

            for n in range(4):
                dve.wait_ge(wv_turned, n + 1)
                nc.vector.tensor_copy(wv_t[:, 2 * n:2 * n + 2, :],
                                      bank[n][:].rearrange("p (a k) -> p a k", a=2)).then_inc(wv_copied, 1)
            take_turned(0)
            take_turned(1)
            for s in range(SETS):
                if s + 2 < SETS:
                    take_turned(s + 2)
                add_bias(s)

        @block.tensor
        def _(pe):
            def turn(s):
                if s >= 4:
                    pe.wait_ge(turned_ready, s - 3)
                else:
                    pe.wait_ge(wv_copied, s + 1)
                for g in range(4):
                    last = nc.tensor.transpose(bank[s % 4][:, P * g:P * g + P],
                                               rows.rearrange("p i (c g) -> p g (i c)", c=CG)[:, 4 * s + g],
                                               ident[:])
                last.then_inc(rows_turned, 1)

            def conv(s):
                pe.wait_ge(turned_ready, s + 1)
                pe.wait_ge(banded_ready, s // 4 + 1)
                if s >= 4:
                    pe.wait_ge(conv_added, s - 3)
                for g in range(4):
                    o = bank[4 + s % 4][:, P * g:P * g + P]
                    cols = turned[:, s % 4, g].rearrange("p s b -> p (s b)")
                    m = banded[:, (s // 4) % 2, 4 * (s % 4) + g]
                    nc.tensor.matmul(o, cols[:, 0:P], m[:, BLK:WIN], start=True, stop=False)
                    last = nc.tensor.matmul(o, cols[:, BATCHES:BATCHES + P], m[:, 0:BLK],
                                            start=False, stop=True)
                last.then_inc(conv_done, 1)

            pe.wait_ge(ident_ready, 1)
            pe.wait_ge(wv_in, 16)
            for n in range(4):
                for a in range(2):
                    for k in range(KC):
                        last = nc.tensor.transpose(bank[n][:, 256 * a + P * k:256 * a + P * k + P],
                                                   wv[:, k, P * (2 * n + a):P * (2 * n + a) + P], ident[:])
                last.then_inc(wv_turned, 1)
            pe.wait_ge(gathered, 16 * BLK)
            turn(0)
            turn(1)
            for s in range(SETS):
                if s + 2 < SETS:
                    turn(s + 2)
                conv(s)


def raw_piece(weights, n):
    w1, w2 = weights
    if n < KC:
        return w1.rearrange("(k p) n -> k p n", p=P)[n]
    return w2.rearrange("(h c p) n -> h p c n", p=P, h=2)[n - KC]


def raw_place(store, n):
    return store[:, n % 3] if n < KC else store[:, n % 3].rearrange("p (c n) -> p c n", n=DIM)


def store_h(sp, h_d, store, b):
    rows = store[b::BATCHES].rearrange("p a n -> p (a n)")[:, 0:BLK * DIM]
    return sp.dma_start(h_d.rearrange("(b s o) c -> s b (o c)", b=BATCHES, o=BLK)[:, b], rows)


def piece(store, n, dst):
    r = store[:, n % 3]
    if n < KC:
        own = NARROW * NARROW_W
        return [(r[:, 0:own].rearrange("p (e w) -> p e w", w=NARROW_W),
                 dst[:, 0:NARROW * MAXW].rearrange("p (e w) -> p e w", w=MAXW)[:, :, 0:NARROW_W]),
                (r[:, own:], dst[:, NARROW * MAXW:])]
    r = r.rearrange("p (c n) -> p c n", n=DIM)
    if n == KC:
        return [(r[:, 0:8].rearrange("p (e c) n -> p e (c n)", c=2),
                 dst[:, 0:NARROW * FC].rearrange("p (e c) n -> p e (c n)", c=FC)[:, :, 0:2 * DIM]),
                (r[:, 8:12], dst[:, NARROW * FC:NARROW * FC + 4])]
    return [(r, dst[:, NARROW * FC + 4:])]


def attend(nc, ctx, sem, bank, ident, base, base0, router_w, w1, w2, h_d, store, h_stored, raw_in,
           table, queue_d, out, second_half, wqk_hi, wqk_lo, wv_t, wo, bo_all,
           w1_parts, w1_hi_ready, w1_lo_ready, w1_zero):
    def sbuf(name, shape, dt=F32):
        return ctx.enter_context(nc.sbuf_tensor(name, shape, dt))

    h_in = sbuf("h_in", [P, 2, TT, DIM])
    res = sbuf("res", [P, 2, TT, DIM])
    xn = sbuf("xn", [P, TT, DIM])
    xt_hi = sbuf("xt_hi", [P, 2, KC, SEQ], F32R)
    xt_lo = sbuf("xt_lo", [P, 2, KC, SEQ], F32R)
    q = second_half.rearrange("p (b t n) -> p b t n", b=2, t=TT)
    q_max = sbuf("q_max", [P, 2, 8])
    q_sum = sbuf("q_sum", [P, 2, 8])
    q_inv = sbuf("q_inv", [P, 2, 2 * TT, 8])
    k_negmax = sbuf("k_negmax", [P, PAIRS])
    k_exps = sbuf("k_exps", [P, 2, SEQ])
    k_sum = sbuf("k_sum", [P, 2, PAIRS])
    k_inv = sbuf("k_inv", [P, PAIRS])
    k = sbuf("k", [P, TT, INNER])
    context = sbuf("context", [P, PAIRS, P])
    g = sbuf("g", [P, PAIRS, DIM])
    m_hi = sbuf("m_hi", [P, KC, DIM], F32R)
    m_lo = sbuf("m_lo", [P, KC, DIM], F32R)
    stats = sbuf("stats", [P, TT, 6])
    mean_var = sbuf("mean_var", [P, TT, 2])
    var_eps = sbuf("var_eps", [P, TT])
    rstd = sbuf("rstd", [P, TT])
    minus_half = sbuf("minus_half", [P, TT])
    stats2 = sbuf("stats2", [P, TT, 6])
    mean_var2 = sbuf("mean_var2", [P, TT, 2])
    var_eps2 = sbuf("var_eps2", [P, TT])
    rstd2 = sbuf("rstd2", [P, TT])
    x2_t = sbuf("x2_t", [P, KC, SEQ])
    logits_t = x2_t[:, 0, 0:P]
    row = sbuf("row", [P, TT, TOPK, ROW])
    rw = xn[0:EXPERTS, 0]
    rw_t = sbuf("rw_t", [P, KC, COLS])
    prob = sbuf("prob", [P, TT, EXPERTS])
    best = sbuf("best", [P, TT, 8])
    best_at = sbuf("best_at", [P, TT, 8], U32)
    best_atf = sbuf("best_atf", [P, TOPK, TT])
    top_sum = sbuf("top_sum", [P, TT])
    which = sbuf("which", [P, TOPK * TT, EXPERTS])
    counted = sbuf("counted", [P, TT * EXPERTS], BF16)
    place = sbuf("place", [P, TT, EXPERTS])
    placed = sbuf("placed", [P, TOPK * TT, EXPERTS])
    slotf = sbuf("slotf", [P, TOPK * TT])
    slot = sbuf("slot", [P, TOPK * TT], U32)
    before = sbuf("before", [P, P], BF16)
    every = sbuf("every", [P, P], BF16)
    expert_no = sbuf("expert_no", [P, EXPERTS])
    token_no = sbuf("token_no", [P, TT])

    loaded = [sem(f"loaded{i}") for i in range(2)]
    stored = [sem(f"stored{i}") for i in range(2)]
    consts_pool, rw_in, rw_turned, rw_copied = (
        sem(n) for n in ("consts_pool", "rw_in", "rw_turned", "rw_copied"))
    ln_chain, stats_ready, var_ready, rstd_ready, xn_ready = (
        sem(n) for n in ("ln_chain", "stats_ready", "var_ready", "rstd_ready", "xn_ready"))
    res_ready, qk_psum, xt_hi_ready, xt_lo_ready, q_chain = (
        sem(n) for n in ("res_ready", "qk_psum", "xt_hi_ready", "xt_lo_ready", "q_chain"))
    q_shifted, q_exp_ready, q_inv_ready, q_ready, k_max_ready = (
        sem(n) for n in ("q_shifted", "q_exp_ready", "q_inv_ready", "q_ready", "k_max_ready"))
    k_exp_ready, k_psum, k_ready, tail_chain, tail_psum = (
        sem(n) for n in ("k_exp_ready", "k_psum", "k_ready", "tail_chain", "tail_psum"))
    ctx_ready, g_ready, m_hi_ready, m_lo_ready, res_added = (
        sem(n) for n in ("ctx_ready", "g_ready", "m_hi_ready", "m_lo_ready", "res_added"))
    stats2_ready, var2_ready, rstd2_ready, row_ready, x2t_ready = (
        sem(n) for n in ("stats2_ready", "var2_ready", "rstd2_ready", "row_ready", "x2t_ready"))
    prob_exp_ready, counted_ready, rank_psum, slots_ready, queued = (
        sem(n) for n in ("prob_exp_ready", "counted_ready", "rank_psum", "slots_ready", "queued"))
    route_chain, logits_psum, logits_ready, dve_passed, pool_passed = (
        sem(n) for n in ("route_chain", "logits_psum", "logits_ready", "dve_passed", "pool_passed"))

    QK_USES, Q_UNITS, TAIL_USES = 2 + 2 * TT + PAIRS, 2 * TT, 12
    LN_LINKS, Q_LINKS, TAIL_LINKS, BEST_LINKS, ROUTE_LINKS = 1, 2 * Q_UNITS, 2, 6, 15

    def qk_bank(use):
        return bank[use % 3]

    def k_bank(c):
        return bank[3 + c % 2]

    def tail_bank(use):
        return bank[5 + use % 3]

    def steps(engine, step):
        b = [Batch(n, n % 2, n // 2) for n in range(BATCHES)]
        step(None, None, b[0], None)
        step(b[0], None, b[1], None)
        step(b[1], b[0], b[2], None)
        with engine.Fori(1, BATCHES // 2) as i:
            even, odd = Batch(i * 2, 0, i), Batch(i * 2 + 1, 1, i)
            step(even, Batch(i * 2 - 1, 1, i - 1), odd, Batch(i * 2 - 2, 0, i - 1))
            step(odd, even, Batch(i * 2 + 2, 0, i + 1), Batch(i * 2 - 1, 1, i - 1))
        step(None, b[BATCHES - 1], None, b[BATCHES - 2])
        step(None, None, None, b[BATCHES - 1])

    with nc.Block() as block:
        @block.sync
        def _(sp):
            sp.dma_start(rw, router_w).then_inc(rw_in, 16)

            @unless_none
            def load(b):
                if not (b.is_first(2)):
                    sp.wait_ge(xn_ready, b.nth(1, -1))
                    sp.wait_ge(res_ready, b.nth(1, -1))
                if b.is_first(3):
                    sp.wait_ge(h_stored[b.n], 16 if b.n < 2 else 16 * (BATCHES - 2))
                first = b.n * SEQ if isinstance(b.n, int) else (b.n % BATCHES) * SEQ
                sp.dma_start(h_in[:, b.par], h_d[bass.ds(first, SEQ), :].rearrange("(t p) c -> p t c", p=P)
                             ).then_inc(loaded[b.par], 16)
                if b.is_first(2) and b.n == 1:
                    for later in range(2, BATCHES):
                        store_h(sp, h_d, store, later).then_inc(h_stored[2], 16)
                if b.is_first(3) and b.n == 2:
                    for n in range(3):
                        sp.dma_start(raw_place(store, n), raw_piece((w1, w2), n)).then_inc(raw_in[n], 16)

            @unless_none
            def store_h2(b):
                sp.wait_ge(res_added, b.nth(2, 2))
                sp.dma_start(out[bass.ds(b.n * SEQ, SEQ), :].rearrange("(t p) c -> p t c", p=P), res[:, b.par]
                             ).then_inc(stored[b.par], 16)

            def step(b, prev, nxt, old):
                load(nxt)
                store_h2(prev)

            steps(sp, step)
            sp.wait_ge(w1_lo_ready, 1)
            sp.dma_start(raw_place(store, 3), raw_piece((w1, w2), 3)).then_inc(raw_in[3], 16)
            sp.wait_ge(table.filler_ready, 1)
            sp.dma_start(out[TOKENS:TOKENS + P, :], table.filler[:, 0:DIM]).then_inc(table.filled, 16)
            sp.dma_start(queue_d[FILLER_ROW:FILLER_ROW + P, :], table.filler[:]).then_inc(table.filled, 16)
            sp.wait_ge(table.ends_ready, 1)
            for e in range(EXPERTS):
                at = sp.value_load(table.end_i[0:1, e:e + 1], min_val=0, max_val=FILLER_ROW)
                sp.dma_start(queue_d[bass.ds(at, P), :], table.filler[:]).then_inc(table.filled, 16)
            for s in stored:
                sp.wait_ge(s, 16 * BATCHES // 2)

        @block.gpsimd
        def _(pool):
            nc.gpsimd.memset(minus_half[:], -0.5).then_inc(consts_pool, 1)
            nc.gpsimd.memset(before[:], 1.0).then_inc(consts_pool, 1)
            nc.gpsimd.memset(every[:], 1.0).then_inc(consts_pool, 1)
            nc.gpsimd.memset(context[:], 0.0).then_inc(consts_pool, 1)
            nc.gpsimd.iota(expert_no[:], [[1, EXPERTS]], base=0, channel_multiplier=0,
                           allow_small_or_imprecise_dtypes=True).then_inc(consts_pool, 1)
            nc.gpsimd.iota(base0[:], [[QROWS, EXPERTS]], base=0, channel_multiplier=0,
                           allow_small_or_imprecise_dtypes=True).then_inc(consts_pool, 1)
            nc.gpsimd.iota(base[:], [[QROWS, EXPERTS]], base=0, channel_multiplier=0,
                           allow_small_or_imprecise_dtypes=True).then_inc(consts_pool, 1)
            nc.gpsimd.iota(token_no[:], [[P, TT]], base=0, channel_multiplier=1,
                           allow_small_or_imprecise_dtypes=True).then_inc(consts_pool, 1)
            nc.gpsimd.memset(table.filler[:], 0.0).then_inc(table.consts, 1)
            nc.gpsimd.memset(table.upto[:], 1.0).then_inc(table.consts, 1)
            nc.gpsimd.iota(table.tile_no[:], [[1, TABLE]], base=0, channel_multiplier=0,
                           allow_small_or_imprecise_dtypes=True).then_inc(table.consts, 1)
            pool.wait_ge(table.consts, 3)
            nc.gpsimd.affine_select(out=table.upto[:], in_=table.upto[:], compare_op=ALU.is_ge, fill=0.0, base=0,
                                    pattern=[[1, EXPERTS], [-1, EXPERTS]], channel_multiplier=0
                                    ).then_inc(table.consts, 1)
            nc.gpsimd.iota(table.filler[:].bitcast(I32)[:, DIM + 1:ROW], [[1, 1]], base=TOKENS, channel_multiplier=1
                           ).then_inc(table.filler_ready, 1)
            pool.wait_ge(consts_pool, 8)
            nc.gpsimd.affine_select(out=before[:], in_=before[:], compare_op=ALU.is_gt, fill=0.0, base=0,
                                    pattern=[[1, P]], channel_multiplier=-1).then_inc(consts_pool, 1)

            @unless_none
            def residual(b):
                pool.wait_ge(loaded[b.par], (b.half + 1) * 16)
                if not (b.is_first(2)):
                    pool.wait_ge(stored[b.par], b.half * 16)
                    pool.wait_ge(row_ready, b.nth(1, -1))
                nc.gpsimd.tensor_tensor(res[:, b.par], h_in[:, b.par],
                                        bo_all[:].unsqueeze(1).to_broadcast([P, TT, DIM]), ALU.add
                                        ).then_inc(res_ready, 1)

            def root(b, mv, ve, r, ready, mid, done):
                wait_apart(pool, ready, b.nth(1, 1), pool_passed)
                nc.gpsimd.tensor_scalar(ve[:], mv[:, :, 1], EPS, None, ALU.add).then_inc(mid, 1)
                pool.wait_ge(mid, b.nth(1, 1))
                nc.gpsimd.tensor_tensor(r[:], ve[:], minus_half[:], ALU.pow).then_inc(done, 1)

            @unless_none
            def root1(b):
                root(b, mean_var, var_eps, rstd, stats_ready, var_ready, rstd_ready)

            @unless_none
            def root2(b):
                root(b, mean_var2, var_eps2, rstd2, stats2_ready, var2_ready, rstd2_ready)

            @unless_none
            def q_norm(b, u):
                pool.wait_ge(q_inv_ready, b.nth(Q_UNITS, u + 1))
                v = q[:, b.par, u // 2, 512 * (u % 2):512 * (u % 2) + 512].rearrange("p (h d) -> p h d", d=DH)
                nc.gpsimd.tensor_tensor(v, v, q_inv[:, b.par, u].unsqueeze(2).to_broadcast([P, 8, DH]), ALU.mult
                                        ).then_inc(q_ready, 1)

            @unless_none
            def enqueue(b):
                wait_apart(pool, slots_ready, b.nth(1, 1), pool_passed)
                for c in range(TOPK):
                    for t in range(TT):
                        pool.indirect_dma_start(
                            out=queue_d, in_=row[:, t, c, :], in_offset=None,
                            out_offset=bass.IndirectOffsetOnAxis(ap=slot[:, TT * c + t:TT * c + t + 1], axis=0)
                        ).then_inc(queued, 16)

            @unless_none
            def w1_pads(last):
                pool.wait_ge(qk_psum, BATCHES * QK_USES)
                pool.wait_ge(tail_psum, last.nth(TAIL_USES, 2))
                for kk in range(KC):
                    for part in range(2):
                        pad = w1_parts[kk][:, part].bitcast(F32)[:, 0:NARROW * MAXW]
                        nc.gpsimd.memset(pad.rearrange("p (e w) -> p e w", w=MAXW)[:, :, NARROW_W:MAXW], 0.0
                                         ).then_inc(w1_zero, 1)

            def step(b, prev, nxt, old):
                enqueue(old)
                if b is None:
                    w1_pads(prev)
                q_norm(b, 0)
                q_norm(b, 1)
                q_norm(b, 2)
                q_norm(b, 3)
                q_norm(b, 4)
                q_norm(b, 5)
                q_norm(b, 6)
                q_norm(b, 7)
                root1(nxt)
                root2(prev)
                residual(nxt)

            steps(pool, step)
            pool.wait_ge(queued, 16 * TOPK * TT * BATCHES)

        @block.scalar
        def _(act):
            def copy(dst, src, waits, done):
                for s, v in waits:
                    act.wait_ge(s, v)
                nc.scalar.activation(dst, src, ACT.Copy).then_inc(done, 1)

            @unless_none
            def xt_high(b, kk):
                copy(xt_hi[:, b.par, kk], qk_bank(kk)[:], [(qk_psum, b.nth(QK_USES, kk + 1))], xt_hi_ready)

            @unless_none
            def q_exps(b, u):
                act.wait_ge(q_shifted, b.nth(Q_UNITS, u + 1))
                v = q[:, b.par, u // 2, 512 * (u % 2):512 * (u % 2) + 512]
                nc.scalar.activation(v, v, ACT.Exp, scale=SCALE).then_inc(q_exp_ready, 1)

            @unless_none
            def k_exp(b, c):
                act.wait_ge(k_max_ready, b.nth(PAIRS, c + 1))
                if c >= 2 or not (b.is_first(1)):
                    act.wait_ge(k_psum, b.nth(PAIRS, c - 1))
                nc.scalar.activation(k_exps[:, c % 2], qk_bank(10 + c)[:], ACT.Exp, bias=k_negmax[:, c:c + 1],
                                     accum_out=k_sum[:, b.par, c:c + 1]).then_inc(k_exp_ready, 1)

            @unless_none
            def k_take(b, c):
                copy(k[:, :, P * c:P * c + P], k_bank(c)[:].rearrange("p (t e) -> p t e", t=TT),
                     [(k_psum, b.nth(PAIRS, c + 1))], k_ready)

            @unless_none
            def g_take(b, n):
                copy(g[:, 2 * n:2 * n + 2], tail_bank(2 + n)[:].rearrange("p (a n) -> p a n", a=2),
                     [(tail_psum, b.nth(TAIL_USES, 3 + n))], g_ready)

            @unless_none
            def m_high(b):
                copy(m_hi[:], tail_bank(6)[:].rearrange("p (a n) -> p a n", a=2),
                     [(tail_psum, b.nth(TAIL_USES, 7))], m_hi_ready)

            @unless_none
            def x2_take(b, kk):
                copy(x2_t[:, kk], tail_bank(9 + kk)[:], [(tail_psum, b.nth(TAIL_USES, 10 + kk))], x2t_ready)

            @unless_none
            def logits_take(b):
                copy(logits_t, tail_bank(11)[:, 2 * P:3 * P], [(logits_psum, b.nth(1, 1))], logits_ready)

            @unless_none
            def prob_exp(b):
                act.wait_ge(tail_psum, b.nth(TAIL_USES, 12))
                logits = tail_bank(11)[:, 0:P].rearrange("p (t e) -> p t e", t=TT)[:, :, 0:EXPERTS]
                nc.scalar.activation(prob[:], logits, ACT.Exp, scale=-1.0).then_inc(prob_exp_ready, 1)

            @unless_none
            def w1_high(last, kk):
                act.wait_ge(raw_in[kk], 16)
                act.wait_ge(qk_psum, BATCHES * QK_USES)
                act.wait_ge(tail_psum, last.nth(TAIL_USES, 2))
                for src, dst in piece(store, kk, w1_parts[kk][:, 0]):
                    done = nc.scalar.activation(dst, src, ACT.Copy)
                done.then_inc(w1_hi_ready, 1)

            def step(b, prev, nxt, old):
                prob_exp(old)
                q_exps(b, 0)
                q_exps(b, 1)
                q_exps(b, 2)
                q_exps(b, 3)
                g_take(prev, 0)
                q_exps(b, 4)
                g_take(prev, 1)
                q_exps(b, 5)
                g_take(prev, 2)
                g_take(prev, 3)
                q_exps(b, 6)
                if b is None:
                    w1_high(prev, 0)
                    w1_high(prev, 1)
                q_exps(b, 7)
                k_exp(b, 0)
                m_high(prev)
                k_exp(b, 1)
                k_take(b, 0)
                k_exp(b, 2)
                k_exp(b, 3)
                k_take(b, 1)
                k_exp(b, 4)
                k_take(b, 2)
                k_exp(b, 5)
                k_take(b, 3)
                x2_take(prev, 0)
                x2_take(prev, 1)
                k_exp(b, 6)
                k_take(b, 4)
                xt_high(nxt, 0)
                xt_high(nxt, 1)
                k_exp(b, 7)
                k_take(b, 5)
                logits_take(prev)
                k_take(b, 6)
                k_take(b, 7)

            steps(act, step)

        @block.vector
        def _(dve):
            dve.wait_ge(rw_turned, 1)
            nc.vector.memset(rw_t[:, :, EXPERTS:COLS], 0.0).then_inc(rw_copied, 1)
            nc.vector.tensor_copy(rw_t[:, :, 0:EXPERTS],
                                  bank[0][:, 0:KC * EXPERTS].rearrange("p (k e) -> p k e", k=KC)
                                  ).then_inc(rw_copied, 1)
            dve.wait_ge(consts_pool, 9)

            def link(ins, chain, b, per, n, apart=False):
                ins.then_inc(chain, 1)
                if apart:
                    wait_apart(dve, chain, b.nth(per, n), dve_passed)
                else:
                    dve.wait_ge(chain, b.nth(per, n))

            @unless_none
            def ln_stats(b):
                dve.wait_ge(loaded[b.par], (b.half + 1) * 16)
                for t in range(TT):
                    last = nc.vector.bn_stats(stats[:, t], h_in[:, b.par, t])
                link(last, ln_chain, b, LN_LINKS, 1, apart=True)
                for t in range(TT):
                    last = nc.vector.bn_aggr(mean_var[:, t], stats[:, t])
                last.then_inc(stats_ready, 1)

            @unless_none
            def ln_apply(b):
                dve.wait_ge(rstd_ready, b.nth(1, 1))
                if not (b.is_first(1)):
                    dve.wait_ge(qk_psum, b.nth(QK_USES, 2 - QK_USES))
                for t in range(TT):
                    last = nc.vector.tensor_scalar(xn[:, t], h_in[:, b.par, t], mean_var[:, t, 0:1], rstd[:, t:t + 1],
                                                   ALU.subtract, ALU.mult)
                last.then_inc(xn_ready, 1)

            @unless_none
            def xt_low(b, kk):
                dve.wait_ge(xt_hi_ready, b.nth(KC, kk + 1))
                nc.vector.tensor_tensor(xt_lo[:, b.par, kk], qk_bank(kk)[:], xt_hi[:, b.par, kk].bitcast(F32),
                                        ALU.subtract).then_inc(xt_lo_ready, 1)

            @unless_none
            def q_shift(b, u):
                dve.wait_ge(qk_psum, b.nth(QK_USES, u + 3))
                src = qk_bank(2 + u)[:].rearrange("p (h d) -> p h d", d=DH)
                link(nc.vector.tensor_reduce(q_max[:, u % 2], src, AX, ALU.max), q_chain, b, Q_LINKS,
                     2 * u + 1 - (u > 0))
                v = q[:, b.par, u // 2, 512 * (u % 2):512 * (u % 2) + 512].rearrange("p (h d) -> p h d", d=DH)
                nc.vector.tensor_tensor(v, src, q_max[:, u % 2].unsqueeze(2).to_broadcast([P, 8, DH]), ALU.subtract
                                        ).then_inc(q_shifted, 1)

            @unless_none
            def q_total(b, u):
                dve.wait_ge(q_exp_ready, b.nth(Q_UNITS, u + 1))
                v = q[:, b.par, u // 2, 512 * (u % 2):512 * (u % 2) + 512].rearrange("p (h d) -> p h d", d=DH)
                link(nc.vector.tensor_reduce(q_sum[:, u % 2], v, AX, ALU.add), q_chain, b, Q_LINKS,
                     min(2 * u + 3, Q_LINKS))
                nc.vector.reciprocal(q_inv[:, b.par, u], q_sum[:, u % 2]).then_inc(q_inv_ready, 1)

            @unless_none
            def k_max(b, c):
                dve.wait_ge(qk_psum, b.nth(QK_USES, 11 + c))
                if not (b.is_first(1)):
                    dve.wait_ge(k_exp_ready, b.nth(PAIRS, c + 1 - PAIRS))
                nc.vector.tensor_reduce(k_negmax[:, c:c + 1], qk_bank(10 + c)[:], AX, ALU.max, negate=True
                                        ).then_inc(k_max_ready, 1)

            @unless_none
            def context_take(b, n):
                if n == 0:
                    dve.wait_ge(k_exp_ready, b.nth(PAIRS, PAIRS))
                    link(nc.vector.reciprocal(k_inv[:], k_sum[:, b.par]), tail_chain, b, TAIL_LINKS, 1)
                dve.wait_ge(tail_psum, b.nth(TAIL_USES, n + 1))
                for half in range(2):
                    r = slice(DH * half, DH * half + DH)
                    src = tail_bank(n)[r, 0:4 * DH].rearrange("p (a d) -> p a d", a=4)
                    last = nc.vector.tensor_tensor(context[r, 4 * n:4 * n + 4, r], src,
                                                   k_inv[r, 4 * n:4 * n + 4].unsqueeze(2).to_broadcast([DH, 4, DH]),
                                                   ALU.mult)
                last.then_inc(ctx_ready, 1)

            @unless_none
            def m_low(b):
                dve.wait_ge(m_hi_ready, b.nth(1, 1))
                nc.vector.tensor_tensor(m_lo[:], tail_bank(6)[:].rearrange("p (a n) -> p a n", a=2),
                                        m_hi[:].bitcast(F32), ALU.subtract).then_inc(m_lo_ready, 1)

            @unless_none
            def add_attention(b):
                dve.wait_ge(res_ready, b.nth(1, 1))
                for n in range(2):
                    dve.wait_ge(tail_psum, b.nth(TAIL_USES, 8 + n))
                    r = res[:, b.par, 2 * n:2 * n + 2]
                    nc.vector.tensor_tensor(r, tail_bank(7 + n)[:].rearrange("p (t c) -> p t c", t=2), r, ALU.add
                                            ).then_inc(res_added, 1)

            @unless_none
            def ln2_stats(b):
                dve.wait_ge(res_added, b.nth(2, 2))
                for t in range(TT):
                    last = nc.vector.bn_stats(stats2[:, t], res[:, b.par, t])
                link(last, tail_chain, b, TAIL_LINKS, 2, apart=True)
                for t in range(TT):
                    last = nc.vector.bn_aggr(mean_var2[:, t], stats2[:, t])
                last.then_inc(stats2_ready, 1)

            @unless_none
            def ln2_apply(b):
                dve.wait_ge(rstd2_ready, b.nth(1, 1))
                if not (b.is_first(1)):
                    dve.wait_ge(queued, b.nth(16 * TOPK * TT, 0))
                for t in range(TT):
                    last = nc.vector.tensor_scalar(row[:, t, :, 0:DIM],
                                                   res[:, b.par, t].unsqueeze(1).to_broadcast([P, TOPK, DIM]),
                                                   mean_var2[:, t, 0:1], rstd2[:, t:t + 1], ALU.subtract, ALU.mult)
                last.then_inc(row_ready, 1)

            @unless_none
            def route_best(b):
                n = [0]

                def then(ins, apart=False):
                    n[0] += 1
                    link(ins, route_chain, b, ROUTE_LINKS, n[0], apart)

                dve.wait_ge(prob_exp_ready, b.nth(1, 1))
                then(nc.vector.tensor_scalar(prob[:], prob[:], 1.0, None, ALU.add))
                then(nc.vector.reciprocal(prob[:], prob[:]), apart=True)
                for t in range(TT):
                    last = nc.vector.max(best[:, t], prob[:, t])
                then(last, apart=True)
                for t in range(TT):
                    last = nc.vector.max_index(best_at[:, t], best[:, t], prob[:, t])
                then(last)
                then(nc.vector.tensor_copy(best_atf[:], best_at[:, :, 0:TOPK].rearrange("p t c -> p c t")))
                full = [P, TOPK * TT, EXPERTS]
                then(nc.vector.tensor_tensor(
                    which[:], expert_no[:].unsqueeze(1).to_broadcast(full),
                    best_atf[:].rearrange("p c t -> p (c t)").unsqueeze(2).to_broadcast(full), ALU.is_equal))
                nc.vector.tensor_tensor(counted[:].rearrange("p (t e) -> p t e", t=TT), which[:, 0:TT],
                                        which[:, TT:2 * TT], ALU.add).then_inc(counted_ready, 1)
                assert n[0] == BEST_LINKS, n[0]

            @unless_none
            def route_slots(b):
                n = [BEST_LINKS]

                def then(ins, apart=False):
                    n[0] += 1
                    link(ins, route_chain, b, ROUTE_LINKS, n[0], apart)

                then(nc.vector.tensor_tensor(top_sum[:], best[:, :, 0], best[:, :, 1], ALU.add))
                then(nc.vector.tensor_scalar(top_sum[:], top_sum[:], 1e-20, None, ALU.add))
                then(nc.vector.reciprocal(top_sum[:], top_sum[:]))
                nc.vector.tensor_tensor(row[:, :, :, DIM], best[:, :, 0:TOPK],
                                        top_sum[:].unsqueeze(2).to_broadcast([P, TT, TOPK]), ALU.mult)
                then(nc.vector.tensor_copy(row[:].bitcast(I32)[:, :, :, DIM + 1],
                                           token_no[:].unsqueeze(2).to_broadcast([P, TT, TOPK])))
                then(nc.vector.tensor_scalar(token_no[:], token_no[:], float(SEQ), None, ALU.add))
                dve.wait_ge(rank_psum, b.nth(1, 1))
                rank = tail_bank(11)[:, P:P + (TT + 1) * EXPERTS].rearrange("p (t e) -> p t e", e=EXPERTS)
                then(nc.vector.tensor_tensor(place[:], rank[:, 0:TT], base[:].unsqueeze(1).to_broadcast(
                    [P, TT, EXPERTS]), ALU.add))
                then(nc.vector.tensor_tensor(base[:], rank[:, TT], base[:], ALU.add))
                for c in range(TOPK):
                    last = nc.vector.tensor_tensor(placed[:, TT * c:TT * c + TT], which[:, TT * c:TT * c + TT],
                                                   place[:], ALU.mult)
                then(last)
                then(nc.vector.tensor_reduce(slotf[:], placed[:], AX, ALU.add))
                nc.vector.tensor_copy(slot[:], slotf[:]).then_inc(slots_ready, 1)
                assert n[0] == ROUTE_LINKS, n[0]

            @unless_none
            def w1_low(last, kk):
                dve.wait_ge(w1_hi_ready, kk + 1)
                hi, lo = (piece(store, kk, w1_parts[kk][:, part]) for part in range(2))
                for (src, high), (_, dst) in zip(hi, lo):
                    done = nc.vector.tensor_tensor(dst, src, high.bitcast(F32), ALU.subtract)
                done.then_inc(w1_lo_ready, 1)

            def step(b, prev, nxt, old):
                q_shift(b, 0)
                route_best(old)
                q_shift(b, 1)
                q_total(b, 0)
                q_shift(b, 2)
                q_total(b, 1)
                context_take(prev, 0)
                route_slots(old)
                context_take(prev, 1)
                if b is None:
                    w1_low(prev, 0)
                q_shift(b, 3)
                q_total(b, 2)
                q_shift(b, 4)
                q_total(b, 3)
                q_shift(b, 5)
                q_total(b, 4)
                q_shift(b, 6)
                q_total(b, 5)
                q_shift(b, 7)
                q_total(b, 6)
                q_total(b, 7)
                k_max(b, 0)
                ln_stats(nxt)
                m_low(prev)
                k_max(b, 1)
                add_attention(prev)
                ln2_stats(prev)
                k_max(b, 2)
                k_max(b, 3)
                ln2_apply(prev)
                if b is None:
                    w1_low(prev, 1)
                k_max(b, 4)
                k_max(b, 5)
                ln_apply(nxt)
                k_max(b, 6)
                k_max(b, 7)
                xt_low(nxt, 0)
                xt_low(nxt, 1)

            steps(dve, step)
            n = [0]

            def chained(ins):
                n[0] += 1
                ins.then_inc(table.chain, 1)
                dve.wait_ge(table.chain, n[0])

            space, at = x2_t[:].rearrange("p k n -> p (k n)"), [0]

            def taken(rows, n):
                at[0] += n
                return space[0:rows, at[0] - n:at[0]]

            passed = taken(1, TABLE * EXPERTS).rearrange("p (t e) -> p t e", e=EXPERTS)
            upto_tiles = taken(P, EXPERTS * EXPERTS).rearrange("p (t e) -> p t e", e=EXPERTS)
            expert_f, start_f, differs, no_rows = (taken(1, TABLE) for _ in range(4))
            chained(nc.vector.tensor_copy(table.end_i[:], base[:]))
            chained(nc.vector.tensor_tensor(table.count[:], base[:], base0[:], ALU.subtract))
            chained(nc.vector.tensor_scalar(table.count[:], table.count[:], float(P - 1), None, ALU.add))
            chained(nc.vector.tensor_copy(table.count_i[:], table.count[:]))
            nc.vector.tensor_scalar(table.count_i[:], table.count_i[:], 7, None, ALU.logical_shift_right
                                    ).then_inc(table.ends_ready, 1)
            dve.wait_ge(table.ends_ready, 1)
            chained(nc.vector.tensor_copy(table.tiles[:], table.count_i[:]))
            dve.wait_ge(table.consts, 4)
            chained(nc.vector.tensor_tensor(upto_tiles, table.upto[:], table.tiles[:].unsqueeze(1).to_broadcast(
                [P, EXPERTS, EXPERTS]), ALU.mult))
            chained(nc.vector.tensor_reduce(table.end[:], upto_tiles, AX, ALU.add))
            full = [1, TABLE, EXPERTS]
            chained(nc.vector.tensor_tensor(passed, table.end[0:1].unsqueeze(1).to_broadcast(full),
                                         table.tile_no[:].unsqueeze(2).to_broadcast(full), ALU.is_le))
            chained(nc.vector.tensor_reduce(expert_f, passed, AX, ALU.add))
            chained(nc.vector.tensor_tensor(passed, passed, table.tiles[0:1].unsqueeze(1).to_broadcast(full),
                                            ALU.mult))
            chained(nc.vector.tensor_reduce(start_f, passed, AX, ALU.add))
            chained(nc.vector.tensor_tensor(start_f, table.tile_no[:], start_f, ALU.subtract))
            chained(nc.vector.tensor_scalar(start_f, start_f, float(P), None, ALU.mult))
            chained(nc.vector.scalar_tensor_tensor(out=start_f, in0=expert_f, scalar=float(QROWS), in1=start_f,
                                                op0=ALU.mult, op1=ALU.add))
            chained(nc.vector.tensor_scalar(table.row_of[:], start_f, float(FILLER_ROW), None, ALU.min))
            chained(nc.vector.tensor_scalar(no_rows, expert_f, float(EXPERTS), None, ALU.is_ge))
            chained(nc.vector.tensor_copy(differs, no_rows))
            chained(nc.vector.tensor_tensor(differs[:, 1:], expert_f[:, 1:], expert_f[:, 0:TABLE - 1], ALU.not_equal))
            chained(nc.vector.tensor_tensor(differs, differs, no_rows, ALU.max))
            chained(nc.vector.tensor_scalar(table.apart[:], differs, 16.0, None, ALU.mult))
            nc.vector.tensor_scalar(table.expert_of[:], expert_f, float(EXPERTS - 1), None, ALU.min
                                    ).then_inc(table.ready, 1)

        @block.tensor
        def _(pe):
            pe.wait_ge(rw_in, 16)
            for kk in range(KC):
                last = nc.tensor.transpose(bank[0][:, EXPERTS * kk:EXPERTS * kk + EXPERTS], rw[:, P * kk:P * kk + P],
                                           ident[0:EXPERTS, 0:EXPERTS])
            last.then_inc(rw_turned, 1)
            pe.wait_ge(rw_copied, 2)
            pe.wait_ge(consts_pool, 9)

            def first(b):
                return b.is_first(1)

            def qk_free(b, use):
                prev = use - 3
                if prev < 0:
                    if first(b):
                        return
                    pe.wait_ge(k_exp_ready, b.nth(PAIRS, prev + 1))
                elif prev < 2:
                    pe.wait_ge(xt_lo_ready, b.nth(KC, prev + 1))
                elif prev < 2 + Q_UNITS:
                    pe.wait_ge(q_shifted, b.nth(Q_UNITS, prev - 1))
                else:
                    pe.wait_ge(k_exp_ready, b.nth(PAIRS, prev - 9))

            TAIL_READS = [(ctx_ready, 2, 1), (ctx_ready, 2, 2), (g_ready, 4, 1), (g_ready, 4, 2),
                          (g_ready, 4, 3), (g_ready, 4, 4), (m_lo_ready, 1, 1), (res_added, 2, 1),
                          (res_added, 2, 2), (x2t_ready, 2, 1), (x2t_ready, 2, 2), (slots_ready, 1, 1)]

            def tail_free(b, use):
                prev = use - 3
                if prev < 0 and first(b):
                    return
                done, per, n = TAIL_READS[prev % TAIL_USES]
                pe.wait_ge(done, b.nth(per, n if prev >= 0 else n - per))

            @unless_none
            def xt(b, kk):
                pe.wait_ge(xn_ready, b.nth(1, 1))
                qk_free(b, kk)
                for t in range(TT):
                    last = nc.tensor.transpose(qk_bank(kk)[:, P * t:P * t + P], xn[:, t, P * kk:P * kk + P], ident[:])
                last.then_inc(qk_psum, 1)

            def split_product(o, pairs):
                n = 0
                for lh, ll, rh, rl in pairs:
                    for a, c in ((lh, rh), (lh, rl), (ll, rh)):
                        n += 1
                        last = nc.tensor.matmul(o, a, c, start=(n == 1), stop=(n == 3 * len(pairs)))
                return last

            @unless_none
            def q_unit(b, u):
                if u == 0:
                    pe.wait_ge(xt_hi_ready, b.nth(KC, KC))
                    pe.wait_ge(xt_lo_ready, b.nth(KC, KC))
                qk_free(b, 2 + u)
                t, c = P * (u // 2), 512 * (u % 2)
                split_product(qk_bank(2 + u)[:], [
                    (xt_hi[:, b.par, kk, t:t + P], xt_lo[:, b.par, kk, t:t + P],
                     wqk_hi[:, kk, c:c + 512], wqk_lo[:, kk, c:c + 512]) for kk in range(KC)]
                ).then_inc(qk_psum, 1)

            @unless_none
            def k_unit(b, c):
                qk_free(b, 10 + c)
                w = slice(INNER + P * c, INNER + P * c + P)
                split_product(qk_bank(10 + c)[:], [
                    (wqk_hi[:, kk, w], wqk_lo[:, kk, w], xt_hi[:, b.par, kk], xt_lo[:, b.par, kk])
                    for kk in range(KC)]).then_inc(qk_psum, 1)

            @unless_none
            def k_turn(b, c):
                pe.wait_ge(k_exp_ready, b.nth(PAIRS, c + 1))
                if c >= 2 or not first(b):
                    pe.wait_ge(k_ready, b.nth(PAIRS, c - 1))
                for t in range(TT):
                    last = nc.tensor.transpose(k_bank(c)[:, P * t:P * t + P], k_exps[:, c % 2, P * t:P * t + P],
                                               ident[:])
                last.then_inc(k_psum, 1)

            @unless_none
            def context_of(b, n):
                pe.wait_ge(q_ready, b.nth(Q_UNITS, Q_UNITS))
                pe.wait_ge(k_ready, b.nth(PAIRS, PAIRS))
                tail_free(b, n)
                for a in range(4):
                    for t in range(TT):
                        for half in range(2):
                            c = P * (4 * n + a) + DH * half
                            last = nc.tensor.matmul(
                                tail_bank(n)[DH * half:DH * half + DH, DH * a:DH * a + DH], k[:, t, c:c + DH],
                                q[:, b.par, t, c:c + DH], start=(t == 0), stop=(t == TT - 1),
                                tile_position=(0, DH * half))
                last.then_inc(tail_psum, 1)

            @unless_none
            def g_of(b, n):
                pe.wait_ge(ctx_ready, b.nth(2, n // 2 + 1))
                tail_free(b, 2 + n)
                for a in range(2):
                    last = nc.tensor.matmul(tail_bank(2 + n)[:, DIM * a:DIM * a + DIM], context[:, 2 * n + a],
                                            wo[:, 2 * n + a], start=True, stop=True)
                last.then_inc(tail_psum, 1)

            @unless_none
            def m_of(b):
                pe.wait_ge(g_ready, b.nth(4, 4))
                tail_free(b, 6)
                for kk in range(KC):
                    for a in range(PAIRS):
                        last = nc.tensor.matmul(tail_bank(6)[:, DIM * kk:DIM * kk + DIM],
                                                wv_t[:, a, P * kk:P * kk + P], g[:, a],
                                                start=(a == 0), stop=(a == PAIRS - 1))
                last.then_inc(tail_psum, 1)

            @unless_none
            def attention_of(b):
                pe.wait_ge(m_hi_ready, b.nth(1, 1))
                pe.wait_ge(m_lo_ready, b.nth(1, 1))
                for n in range(2):
                    tail_free(b, 7 + n)
                    for a in range(2):
                        t = P * (2 * n + a)
                        last = split_product(tail_bank(7 + n)[:, DIM * a:DIM * a + DIM], [
                            (xt_hi[:, b.par, kk, t:t + P], xt_lo[:, b.par, kk, t:t + P], m_hi[:, kk], m_lo[:, kk])
                            for kk in range(KC)])
                    last.then_inc(tail_psum, 1)

            @unless_none
            def x2_turn(b):
                pe.wait_ge(row_ready, b.nth(1, 1))
                for kk in range(KC):
                    tail_free(b, 9 + kk)
                    for t in range(TT):
                        last = nc.tensor.transpose(tail_bank(9 + kk)[:, P * t:P * t + P],
                                                   row[:, t, 0, P * kk:P * kk + P], ident[:])
                    last.then_inc(tail_psum, 1)

            @unless_none
            def router(b):
                pe.wait_ge(x2t_ready, b.nth(KC, KC))
                tail_free(b, 11)
                for kk in range(KC):
                    for t in range(TT):
                        last = nc.tensor.matmul(tail_bank(11)[COLS * t:COLS * t + COLS, 2 * P:3 * P], rw_t[:, kk],
                                                x2_t[:, kk, P * t:P * t + P], start=(kk == 0), stop=(kk == KC - 1),
                                                tile_position=(0, COLS * t))
                last.then_inc(logits_psum, 1)

            @unless_none
            def router_turn(b):
                pe.wait_ge(logits_ready, b.nth(1, 1))
                nc.tensor.transpose(tail_bank(11)[:, 0:P], logits_t, ident[:]).then_inc(tail_psum, 1)

            @unless_none
            def ranks(b):
                pe.wait_ge(counted_ready, b.nth(1, 1))
                for t in range(TT + 1):
                    o = tail_bank(11)[:, P + EXPERTS * t:P + EXPERTS * t + EXPERTS]
                    terms = [(every, s) for s in range(t)] + [(before, t)] * (t < TT)
                    for n, (a, s) in enumerate(terms):
                        last = nc.tensor.matmul(o, a[:], counted[:, EXPERTS * s:EXPERTS * s + EXPERTS],
                                                start=(n == 0), stop=(n == len(terms) - 1))
                last.then_inc(rank_psum, 1)

            def step(b, prev, nxt, old):
                q_unit(b, 0)
                router_turn(old)
                q_unit(b, 1)
                q_unit(b, 2)
                context_of(prev, 0)
                ranks(old)
                context_of(prev, 1)
                q_unit(b, 3)
                q_unit(b, 4)
                q_unit(b, 5)
                g_of(prev, 0)
                g_of(prev, 1)
                q_unit(b, 6)
                g_of(prev, 2)
                g_of(prev, 3)
                q_unit(b, 7)
                k_unit(b, 0)
                m_of(prev)
                k_unit(b, 1)
                k_turn(b, 0)
                attention_of(prev)
                k_unit(b, 2)
                k_turn(b, 1)
                k_unit(b, 3)
                k_unit(b, 4)
                k_turn(b, 2)
                k_unit(b, 5)
                k_turn(b, 3)
                x2_turn(prev)
                k_unit(b, 6)
                k_turn(b, 4)
                k_unit(b, 7)
                xt(nxt, 0)
                xt(nxt, 1)
                k_turn(b, 5)
                router(prev)
                k_turn(b, 6)
                k_turn(b, 7)

            steps(pe, step)


def experts(nc, ctx, sem, bank, ident, store, raw_in, table, queue_d, out, w1_parts, w1_lo_ready, w1_zero):
    def sbuf(name, shape, dt=F32):
        return ctx.enter_context(nc.sbuf_tensor(name, shape, dt))

    w2_hi = sbuf("w2_hi", [P, EXPERTS * FC, DIM], F32R)
    w2_lo = sbuf("w2_lo", [P, EXPERTS * FC, DIM], F32R)
    rows = sbuf("queue_rows", [P, SLOTS, ROW])
    x_hi = sbuf("x_hi", [P, 2, DIM], F32R)
    x_lo = sbuf("x_lo", [P, 2, DIM], F32R)
    relu = sbuf("relu", [P, 2, MAXW])
    act_w = sbuf("act_w", [P, 2, MAXW])
    a_hi = sbuf("a_hi", [P, 2, MAXW], F32R)
    a_lo = sbuf("a_lo", [P, 2, MAXW], F32R)
    y = sbuf("y", [P, 2, DIM])
    rows_in = [sem(f"rows_in{i}") for i in range(SLOTS)]
    pads_zero = sem("pads_zero")
    w2_hi_ready, w2_lo_ready, x_turned, x_hi_ready, x_lo_ready, up_done, relu_ready, act_ready = (sem(n) for n in (
        "w2_hi_ready", "w2_lo_ready", "x_turned", "x_hi_ready", "x_lo_ready", "up_done", "relu_ready", "act_ready"))
    act_turned, a_hi_ready, a_lo_ready, down_done, y_ready, pool_passed3 = (sem(n) for n in (
        "act_turned", "a_hi_ready", "a_lo_ready", "down_done", "y_ready", "pool_passed3"))
    halves_zero = sem("halves_zero")
    added = [sem(f"added{i}") for i in range(2)]

    def need(engine, s, value):
        if not isinstance(value, int) or value > 0:
            engine.wait_ge(s, value)

    def all_turns(engine, step):
        def of_turn(turn):
            last = engine.value_load(table.expert_of[0:1, bass.ds(turn * SLOTS + SLOTS - 1, 1)], min_val=0,
                                     max_val=EXPERTS - 1)
            with engine.If(last < NARROW):
                for u in range(SLOTS):
                    step(turn, u, NARROW_W)
            with engine.Else():
                for u in range(SLOTS):
                    step(turn, u, MAXW)

        of_turn(0)
        with engine.Fori(1, TILES // SLOTS) as i:
            of_turn(i)

    with nc.Block() as block:
        @block.sync
        def _(sp):
            sp.wait_ge(table.ready, 1)
            sp.wait_ge(table.filled, 16 * (EXPERTS + 2))

            def load(j, u, turn):
                at = sp.value_load(table.row_of[0:1, bass.ds(j, 1)], min_val=0, max_val=FILLER_ROW)
                if turn is not None:
                    sp.wait_ge(added[u % 2], (turn * (SLOTS // 2) + u // 2 + 1) * 16)
                sp.dma_start(rows[:, u], queue_d[bass.ds(at, P), :]).then_inc(rows_in[u], 16)

            for j in range(SLOTS):
                load(j, j, None)
            with sp.Fori(1, TILES // SLOTS) as i:
                for u in range(SLOTS):
                    load(i * SLOTS + u, u, i - 1)
            for u in range(AHEAD):
                load(TILES + u, u, TILES // SLOTS - 1)

        @block.gpsimd
        def _(pool):
            for a in (act_w[:], a_hi[:].bitcast(F32), a_lo[:].bitcast(F32)):
                nc.gpsimd.memset(a[:, :, NARROW_W:MAXW], 0.0).then_inc(halves_zero, 1)
            for w in (w2_hi, w2_lo):
                pad = w[:].bitcast(F32)[:, 0:NARROW * FC].rearrange("p (e c) n -> p e (c n)", c=FC)
                nc.gpsimd.memset(pad[:, :, 2 * DIM:], 0.0).then_inc(pads_zero, 1)

            def add(j, u, pair):
                wait_apart(pool, y_ready, j + 1, pool_passed3)
                if not isinstance(j, int) or j >= 2:
                    wait_apart(pool, added[u % 2], pair * 16, pool_passed3)
                if isinstance(j, int) and 1 <= j <= 2:
                    wait_apart(pool, added[1 - u % 2], 16, pool_passed3)
                elif not isinstance(j, int) or j > 2:
                    differs16 = pool.value_load(table.apart[0:1, bass.ds(j, 1)], min_val=0, max_val=16)
                    wait_apart(pool, added[1 - u % 2], (pair + u % 2 - 1) * 16 + differs16, pool_passed3)
                pool.indirect_dma_start(
                    out=out, in_=y[:, u % 2, :], in_offset=None, compute_op=ALU.add,
                    out_offset=bass.IndirectOffsetOnAxis(ap=rows[:, u, DIM + 1:ROW].bitcast(U32), axis=0)
                ).then_inc(added[u % 2], 16)

            pool.wait_ge(table.ready, 1)
            for j in range(SLOTS):
                add(j, j, j // 2)
            with pool.Fori(1, TILES // SLOTS) as i:
                for u in range(SLOTS):
                    add(i * SLOTS + u, u, i * (SLOTS // 2) + u // 2)
            for s in added:
                pool.wait_ge(s, 16 * TILES // 2)

        @block.scalar
        def _(act):
            def w2_high(n):
                act.wait_ge(raw_in[n], 16)
                for src, dst in piece(store, n, w2_hi):
                    last = nc.scalar.activation(dst, src, ACT.Copy)
                last.then_inc(w2_hi_ready, 1)

            def x_high(j, u):
                need(act, x_turned, j + 1)
                need(act, up_done, j - 1)
                nc.scalar.activation(x_hi[:, u % 2], bank[u % 2][:, 0:DIM], ACT.Copy).then_inc(x_hi_ready, 1)

            def take_relu(j, u, width):
                need(act, up_done, j + 1)
                need(act, act_ready, j - 1)
                nc.scalar.activation(relu[:, u % 2, 0:width], bank[2 + u % 2][:, 0:width], ACT.Relu
                                     ).then_inc(relu_ready, 1)

            def act_high(j, u, width):
                need(act, act_turned, j + 1)
                need(act, down_done, j - 1)
                nc.scalar.activation(a_hi[:, u % 2, 0:width], bank[4 + u % 2][:, 0:width], ACT.Copy
                                     ).then_inc(a_hi_ready, 1)

            def take_y(j, u, pair):
                need(act, down_done, j + 1)
                need(act, added[u % 2], pair * 16)
                nc.scalar.activation(y[:, u % 2], bank[6 + u % 2][:, 0:DIM], ACT.Copy).then_inc(y_ready, 1)

            def step(turn, u, width):
                j, pair = turn * SLOTS + u, turn * (SLOTS // 2) + u // 2
                take_relu(j, u, width)
                x_high(j + AHEAD, u)
                if not isinstance(j, int) or j >= 1:
                    act_high(j - 1, u + 1, width)
                if not isinstance(j, int) or j >= 2:
                    take_y(j - 2, u, pair - 1)

            w2_high(2)
            x_high(0, 0)
            x_high(1, 1)
            w2_high(3)
            act.wait_ge(table.ready, 1)
            all_turns(act, step)
            act_high(TILES - 1, 1, MAXW)
            take_y(TILES - 2, 0, TILES // 2 - 1)
            take_y(TILES - 1, 1, TILES // 2 - 1)

        @block.vector
        def _(dve):
            def w2_low(n):
                dve.wait_ge(w2_hi_ready, n - 1)
                for (src, hi), (_, dst) in zip(piece(store, n, w2_hi), piece(store, n, w2_lo)):
                    last = nc.vector.tensor_tensor(dst, src, hi.bitcast(F32), ALU.subtract)
                last.then_inc(w2_lo_ready, 1)

            def x_low(j, u):
                need(dve, x_hi_ready, j + 1)
                nc.vector.tensor_tensor(x_lo[:, u % 2], bank[u % 2][:, 0:DIM], x_hi[:, u % 2].bitcast(F32),
                                        ALU.subtract).then_inc(x_lo_ready, 1)

            def square(j, u, width):
                need(dve, relu_ready, j + 1)
                need(dve, act_turned, j - 1)
                nc.vector.scalar_tensor_tensor(out=act_w[:, u % 2, 0:width], in0=relu[:, u % 2, 0:width],
                                               scalar=rows[:, u, DIM:DIM + 1], in1=relu[:, u % 2, 0:width],
                                               op0=ALU.mult, op1=ALU.mult).then_inc(act_ready, 1)

            def act_low(j, u, width):
                need(dve, a_hi_ready, j + 1)
                nc.vector.tensor_tensor(a_lo[:, u % 2, 0:width], bank[4 + u % 2][:, 0:width],
                                        a_hi[:, u % 2, 0:width].bitcast(F32), ALU.subtract).then_inc(a_lo_ready, 1)

            def step(turn, u, width):
                j = turn * SLOTS + u
                square(j, u, width)
                x_low(j + AHEAD, u)
                if not isinstance(j, int) or j >= 1:
                    act_low(j - 1, u + 1, width)

            w2_low(2)
            x_low(0, 0)
            x_low(1, 1)
            w2_low(3)
            dve.wait_ge(table.ready, 1)
            all_turns(dve, step)
            act_low(TILES - 1, 1, MAXW)

        @block.tensor
        def _(pe):
            def x_turn(j, u, slot, turn):
                need(pe, rows_in[slot], (turn + 1) * 16)
                need(pe, x_lo_ready, j - 1)
                for k in range(KC):
                    last = nc.tensor.transpose(bank[u % 2][:, P * k:P * k + P], rows[:, slot, P * k:P * k + P],
                                               ident[:])
                last.then_inc(x_turned, 1)

            def split_product(o, pairs, parts):
                n = 0
                for lh, ll, rh, rl in pairs:
                    for a, c in ((lh, rh), (lh, rl), (ll, rh)):
                        n += 1
                        last = nc.tensor.matmul(o, a, c, start=(n == 1), stop=(n == parts))
                return last

            def up(j, u, e, width):
                need(pe, x_lo_ready, j + 1)
                need(pe, act_ready, j - 1)
                w = bass.ds(e * MAXW, width)
                split_product(bank[2 + u % 2][:, 0:width], [
                    (x_hi[:, u % 2, P * k:P * k + P], x_lo[:, u % 2, P * k:P * k + P], w1_parts[k][:, 0, w],
                     w1_parts[k][:, 1, w])
                    for k in range(KC)], 3 * KC).then_inc(up_done, 1)

            def act_turn(j, u, width):
                need(pe, act_ready, j + 1)
                need(pe, a_lo_ready, j - 1)
                for f in range(width // P):
                    last = nc.tensor.transpose(bank[4 + u % 2][:, P * f:P * f + P], act_w[:, u % 2, P * f:P * f + P],
                                               ident[:])
                last.then_inc(act_turned, 1)

            def down(j, u, e, width):
                chunks = width // P
                need(pe, a_lo_ready, j + 1)
                need(pe, y_ready, j - 1)
                hi, lo = (w[:].rearrange("p c n -> p (c n)") for w in (w2_hi, w2_lo))
                at = [bass.ds(e * (FC * DIM) + f * DIM, DIM) for f in range(chunks)]
                split_product(bank[6 + u % 2][:, 0:DIM], [
                    (a_hi[:, u % 2, P * f:P * f + P], a_lo[:, u % 2, P * f:P * f + P], hi[:, at[f]], lo[:, at[f]])
                    for f in range(chunks)], 3 * chunks).then_inc(down_done, 1)

            def load_expert(j):
                return pe.value_load(table.expert_of[0:1, bass.ds(j, 1)], min_val=0, max_val=EXPERTS - 1)

            def step(turn, u, width):
                j = turn * SLOTS + u
                if u == 0:
                    e[0] = load_expert(j)
                up(j, u, e[u], width)
                if u + 1 < SLOTS:
                    e[u + 1] = load_expert(j + 1)
                x_turn(j + AHEAD, u, (u + AHEAD) % SLOTS, turn + (u + AHEAD) // SLOTS)
                if not isinstance(j, int) or j >= 1:
                    act_turn(j - 1, u + 1, width)
                if isinstance(j, int) and j == 2:
                    pe.wait_ge(w2_lo_ready, 2)
                    pe.wait_ge(pads_zero, 2)
                if not isinstance(j, int) or j >= 2:
                    down(j - 2, u, e[u - 2] if u >= 2 else load_expert(j - 2), width)

            e = {}
            x_turn(0, 0, 0, 0)
            x_turn(1, 1, 1, 0)
            pe.wait_ge(table.ready, 1)
            pe.wait_ge(w1_lo_ready, KC)
            pe.wait_ge(w1_zero, 2 * KC)
            pe.wait_ge(halves_zero, 3)
            all_turns(pe, step)
            act_turn(TILES - 1, 1, MAXW)
            for u in range(2):
                down(TILES - 2 + u, u, load_expert(TILES - 2 + u), MAXW)


_INS = ['x', 'L0_tok_embed_table', 'L0_tok_conv_w', 'L0_tok_conv_b', 'L0_attn_w_qkv', 'L0_attn_w_out',
        'L0_attn_b_out', 'L0_ffn_router_w', 'L0_ffn_w1', 'L0_ffn_w2']


def kernel(**inputs):
    import numpy as np
    import concourse.bacc as bacc
    from concourse.bass_utils import run_bass_kernel_spmd

    nc = bacc.Bacc("TRN2", target_bir_lowering=False, num_devices=1)
    arrays, args = {}, []
    for name in _INS:
        a = np.ascontiguousarray(inputs[name])
        if name == "x":
            a = np.concatenate([a[:, SEQ - PAD:], a[:, :SEQ - PAD]], axis=1)
            a = np.ascontiguousarray(a.reshape(BATCHES, NBLK, BLK).transpose(1, 0, 2).reshape(P, BLK))
        arrays[f"in_{name}"] = a
        args.append(nc.dram_tensor(f"in_{name}", a.shape, mybir.dt.from_np(a.dtype), kind="ExternalInput").ap())
    out = nc.dram_tensor("out", (TOKENS + P, DIM), F32, kind="ExternalOutput").ap()
    tower(nc, *args, out)
    r = run_bass_kernel_spmd(nc, [arrays], core_ids=[0])
    return r.results[0]["out"][:TOKENS].reshape(BATCHES, SEQ, DIM)
```
